# Optimizing a Trainium2 kernel written in Bass

```python
import numpy as np
import jax
import jax.numpy as jnp

def _softmax(x, axis=-1):
    return jax.nn.softmax(x, axis=axis)

def _gelu(x):
    return jax.nn.gelu(x, approximate=True)

def _silu(x):
    return jax.nn.silu(x)

def _sigmoid(x):
    return jax.nn.sigmoid(x)

def _layernorm(x, axis=-1, eps=1e-05):
    m = jnp.mean(x, axis=axis, keepdims=True)
    v = jnp.var(x, axis=axis, keepdims=True)
    return (x - m) / jnp.sqrt(v + eps)

def _scatter_add(tgt, idx, src, axis=0):
    return tgt.at[idx].add(src)

def _segment_sum(src, seg, n):
    return jax.ops.segment_sum(src, seg, n)
kernel_name = 'mk_vit_tower_postln_d1_tok_img768_r4_0dd60a'

def setup_inputs(seed: int=0):
    np.random.seed(seed)
    _w = jnp.asarray

    def _rec_inputs():
        import jax
        import jax.numpy as jnp
        _rk = jax.random.key(seed)
        x = 127.472 + 73.6052 * jax.random.normal(jax.random.fold_in(_rk, 1), (64, 224, 224, 3), jnp.float32)
        return x
    x = _rec_inputs()

    def _L0_tok_setup():
        import jax, jax.numpy as jnp
        import numpy as np
        B, H, W_IMG, C = (128, 224, 224, 3)
        P = 16
        NP = H // P * (W_IMG // P)
        D = P * P * C
        PROJ = 192

        def _img2patch(images):
            b = images.shape[0]
            x = images.reshape(b, H // P, P, W_IMG // P, P, C)
            x = x.transpose(0, 1, 3, 2, 4, 5)
            return x.reshape(b, NP, D)
        key = jax.random.key(seed)
        k1, k2, k3, k4 = jax.random.split(key, 4)
        images = jax.random.uniform(k1, (B, H, W_IMG, C), dtype=jnp.float32) * 255.0
        W = jax.random.normal(k2, (D, PROJ), dtype=jnp.float32) * 0.02
        b = jnp.zeros((PROJ,), dtype=jnp.float32)
        class_token = jax.random.normal(k3, (PROJ,), dtype=jnp.float32) * 0.02
        pos_emb = jax.random.normal(k4, (NP + 1, PROJ), dtype=jnp.float32) * 0.02
        return {'images': images, 'W': W, 'b': b, 'class_token': class_token, 'pos_emb': pos_emb}
    _L0_tok_all = _L0_tok_setup()
    _L0_tok_in = {k: v for k, v in _L0_tok_all.items() if k in ('W', 'b', 'class_token', 'pos_emb')}
    del _L0_tok_all

    def _L0_attn_setup():
        import math
        import jax, jax.numpy as jnp
        import numpy as np
        B, T, C, NH = (2, 1024, 192, 12)
        HS = C // NH
        key = jax.random.key(seed)
        k1, k2, k3 = jax.random.split(key, 3)
        x = jax.random.normal(k1, (B, T, C), dtype=jnp.float32)
        w_attn = jax.random.normal(k2, (C, 3 * C), dtype=jnp.float32) * 0.02
        b_attn = jnp.zeros((3 * C,), dtype=jnp.float32)
        w_proj = jax.random.normal(k3, (C, C), dtype=jnp.float32) * 0.02
        b_proj = jnp.zeros((C,), dtype=jnp.float32)
        return {'x': x, 'w_attn': w_attn, 'b_attn': b_attn, 'w_proj': w_proj, 'b_proj': b_proj}
    _L0_attn_all = _L0_attn_setup()
    _L0_attn_in = {k: v for k, v in _L0_attn_all.items() if k in ('w_attn', 'b_attn', 'w_proj', 'b_proj')}
    del _L0_attn_all

    def _L0_ffn_setup():
        import jax, jax.numpy as jnp
        import numpy as np
        E = 8
        TOP_K = 2
        CAP_RATIO = 1.2
        key = jax.random.key(seed)
        k1, k2, k3, k4 = jax.random.split(key, 4)
        B, L, D, H = (2, 512, 192, 512)
        x = jax.random.normal(k1, (B, L, D), dtype=jnp.float32)
        Wg = jax.random.normal(k2, (D, E), dtype=jnp.float32) * 0.02
        W1 = jax.random.normal(k3, (E, D, 2 * H), dtype=jnp.float32) * 0.02
        W2 = jax.random.normal(k4, (E, H, D), dtype=jnp.float32) * 0.02
        return {'x': x, 'Wg': Wg, 'W1': W1, 'W2': W2}
    _L0_ffn_all = _L0_ffn_setup()
    _L0_ffn_in = {k: v for k, v in _L0_ffn_all.items() if k in ('Wg', 'W1', 'W2')}
    del _L0_ffn_all
    return {'x': x, 'L0_tok_W': _L0_tok_in['W'], 'L0_tok_b': _L0_tok_in['b'], 'L0_tok_class_token': _L0_tok_in['class_token'], 'L0_tok_pos_emb': _L0_tok_in['pos_emb'], 'L0_attn_w_attn': _L0_attn_in['w_attn'], 'L0_attn_b_attn': _L0_attn_in['b_attn'], 'L0_attn_w_proj': _L0_attn_in['w_proj'], 'L0_attn_b_proj': _L0_attn_in['b_proj'], 'L0_ffn_Wg': _L0_ffn_in['Wg'], 'L0_ffn_W1': _L0_ffn_in['W1'], 'L0_ffn_W2': _L0_ffn_in['W2']}

def reference(x, L0_tok_W, L0_tok_b, L0_tok_class_token, L0_tok_pos_emb, L0_attn_w_attn, L0_attn_b_attn, L0_attn_w_proj, L0_attn_b_proj, L0_ffn_Wg, L0_ffn_W1, L0_ffn_W2):
    import jax
    import jax.numpy as jnp

    def _L0_tok_ref(images, W, b, class_token, pos_emb):
        import jax, jax.numpy as jnp
        import numpy as np
        B, H, W_IMG, C = (128, 224, 224, 3)
        P = 16
        NP = H // P * (W_IMG // P)
        D = P * P * C
        PROJ = 192

        def _img2patch(images):
            b = images.shape[0]
            x = images.reshape(b, H // P, P, W_IMG // P, P, C)
            x = x.transpose(0, 1, 3, 2, 4, 5)
            return x.reshape(b, NP, D)
        x = images / 255.0
        patches = _img2patch(x)
        proj = jnp.einsum('bnd,de->bne', patches, W) + b
        cls = jnp.broadcast_to(class_token, (images.shape[0], 1, PROJ))
        emb = jnp.concatenate([cls, proj], axis=1) + pos_emb
        return emb

    def _L0_attn_ref(x, w_attn, b_attn, w_proj, b_proj):
        import math
        import jax, jax.numpy as jnp
        import numpy as np
        B, T, C, NH = (2, 1024, 192, 12)
        HS = C // NH
        Bx, Tx, Cx = x.shape
        qkv = x @ w_attn + b_attn
        q, k, v = jnp.split(qkv, 3, axis=-1)
        q = q.reshape(Bx, Tx, NH, HS).transpose(0, 2, 1, 3)
        k = k.reshape(Bx, Tx, NH, HS).transpose(0, 2, 1, 3)
        v = v.reshape(Bx, Tx, NH, HS).transpose(0, 2, 1, 3)
        att = jnp.einsum('bhqd,bhkd->bhqk', q, k) * (1.0 / math.sqrt(HS))
        causal = jnp.tril(jnp.ones((Tx, Tx), dtype=bool))
        att = jnp.where(causal[None, None, :, :], att, -jnp.inf)
        att = jax.nn.softmax(att, axis=-1)
        y = jnp.einsum('bhqk,bhkd->bhqd', att, v)
        y = y.transpose(0, 2, 1, 3).reshape(Bx, Tx, Cx)
        y = y @ w_proj + b_proj
        return y

    def _L0_ffn_ref(x, Wg, W1, W2):
        import jax, jax.numpy as jnp
        import numpy as np
        E = 8
        TOP_K = 2
        CAP_RATIO = 1.2
        B, L, D = x.shape
        H = W2.shape[1]
        xf = x.reshape(-1, D)
        N = xf.shape[0]
        capacity = int(CAP_RATIO * N / E)
        logits = xf @ Wg
        scores, idx = jax.lax.top_k(logits, TOP_K)
        weights = jax.nn.softmax(scores, axis=-1)
        xpad = jnp.concatenate([xf, jnp.zeros((1, D), xf.dtype)], axis=0)
        wpad_zero = jnp.zeros((1,), weights.dtype)
        out = jnp.zeros((N, D), x.dtype)
        for k in range(TOP_K):
            ik = idx[:, k]
            onehot = ik[:, None] == jnp.arange(E)[None, :]
            pos = jnp.cumsum(onehot, axis=0) - 1
            posk = jnp.take_along_axis(pos, ik[:, None], axis=1)[:, 0]
            keep = posk < capacity
            buf = jnp.full((E, capacity), N, dtype=jnp.int32)
            buf = buf.at[ik, posk].set(jnp.arange(N, dtype=jnp.int32), mode='drop')
            xg = xpad[buf]
            h = jnp.einsum('ecd,edh->ech', xg, W1)
            act = h[..., :H] * jax.nn.silu(h[..., H:])
            ye = jnp.einsum('ech,ehd->ecd', act, W2)
            wk = jnp.where(keep, weights[:, k], 0.0)
            w_buf = jnp.concatenate([wk, wpad_zero])[buf]
            out = out.at[buf.reshape(-1)].add((w_buf[..., None] * ye).reshape(E * capacity, D), mode='drop')
        return out.reshape(B, L, D)
    h = _L0_tok_ref(x, L0_tok_W, L0_tok_b, L0_tok_class_token, L0_tok_pos_emb)
    h = _layernorm(h + _L0_attn_ref(h, L0_attn_w_attn, L0_attn_b_attn, L0_attn_w_proj, L0_attn_b_proj), axis=-1)
    h = _layernorm(h + _L0_ffn_ref(h, L0_ffn_Wg, L0_ffn_W1, L0_ffn_W2), axis=-1)
    return h

_drawn_inputs = setup_inputs


def setup_inputs(seed=0):
    import zlib

    import numpy as np

    out = dict(_drawn_inputs(seed))
    spreads = {'L0_tok_b': (0.0, 0.1), 'L0_attn_b_attn': (0.0, 0.1), 'L0_attn_b_proj': (0.0, 0.1)}
    factors = {'L0_tok_class_token': 4.414, 'L0_ffn_Wg': 7.245, 'L0_ffn_W1': 8.0, 'L0_ffn_W2': 8.0}
    for name, (base, spread) in spreads.items():
        noise = np.random.default_rng([zlib.crc32(name.encode()), seed]).standard_normal(out[name].shape)
        drawn = base * np.exp(spread * noise) if base else spread * noise
        out[name] = jnp.asarray(drawn.astype(out[name].dtype))
    for name, factor in factors.items():
        out[name] = (out[name] * factor).astype(out[name].dtype)
    return out
```

```python
from contextlib import ExitStack

import concourse.bass as bass
from concourse import mybir

F32 = mybir.dt.float32
F32R = mybir.dt.float32r
F16 = mybir.dt.float16
BF16 = mybir.dt.bfloat16
I32 = mybir.dt.int32
U32 = mybir.dt.uint32
ALU = mybir.AluOpType
ACT = mybir.ActivationFunctionType
AX = mybir.AxisListType

P = 128
B, T, C = 64, 197, 192
N = B * T
NH, HD = 12, 16
KT = 768 // P
C2 = C - P
NPAIR = B // 2
TI = T + 1
TP = 2 * TI
T1 = TI - P
STEPS = NH
NSTEP = NPAIR * STEPS
E, K2 = 8, 2
HID = 512
CAP = int(1.2 * N / E)
TILE3 = 3 * P
SEG = -(-CAP // TILE3) * TILE3
NSLOT = E * K2 * SEG
ROW = C + 2
FAR = 1.0e6
EPS = 1e-5
SCALE = HD ** -0.5
VW = HD + 1
HM = HID // P
WCOLS = 2 * 2 * HID + HM * C
NWORDS = 256
TRIES = 5

TILES = [(im, hf, im * TI + hf * P, T1 if hf else P) for im in range(2) for hf in range(2)]
REAL = [T - P if hf else P for _, hf, _, _ in TILES]

PIECES = [
    (0, 1, "E0", 0), (1, 1, "E1", 1), (2, 1, "TX0", 0), (2, 1, "TX1", 1),
    (3, 1, "QK0", 0), (3, 1, "QK1", 1), (4, 3, "TY0", 0), (4, 3, "TY1", 1),
    (4, 1, "QK2", 0), (5, 3, "PR0", 1), (5, 1, "SL0", 0), (5, 1, "SL1", 1), (6, 3, "PR1", 0),
    (6, 1, "SL2", 1), (6, 1, "SL3", 0), (7, 1, "SL4", 1), (7, 1, "SL5", 0),
    (8, 3, "TR0", 1), (8, 3, "TR1", 0), (8, 1, "SL6", 1), (8, 1, "SL7", 0),
    (9, 3, "LG", 1), (9, 1, "SL8", 0), (9, 1, "SL9", 1), (10, 1, "SL10", 0), (10, 1, "SL11", 1),
    (11, 3, "RT", 0), (11, 1, "V0", 1), (11, 1, "V1", 0),
]


def stages_of(i):
    return tuple(k for k in (1, 2, 3, 4) if 0 <= i - (k - 1) < NPAIR)


def uses(bank, stages, before=None):
    names = [n for _, _, n, _ in PIECES]
    upto = names.index(before) if before else len(names)
    return sum(1 for _, st, _, b in PIECES[:upto] if b == bank and st in stages)


def uses_before(i, bank):
    if isinstance(i, int):
        return sum(uses(bank, stages_of(n)) for n in range(i))
    return i * uses(bank, (1, 3)) + (uses_before(2, bank) - 2 * uses(bank, (1, 3)))


def run_bodies(eng, body):
    for i in range(4):
        body(i, i // 2, i % 2, stages_of(i))
    with eng.Fori(2, NPAIR // 2) as it:
        for par in range(2):
            body(it * 2 + par, it, par, (1, 2, 3, 4))
    for i in range(NPAIR, NPAIR + 3):
        body(i, i // 2, i % 2, stages_of(i))


def wait(eng, sem, value):
    if not (isinstance(value, int) and value <= 0):
        eng.wait_ge(sem, value)


class Words:

    def __init__(self, eng, words):
        self.eng, self.words, self.n = eng, words, 0

    def wait(self, *waits):
        for sem, value in waits:
            wait(self.eng, sem, value)
        self.n += 1
        w = self.words
        self.eng.tensor_tensor(w[:, self.n:self.n + 1], w[:, 0:1], w[:, 0:1], ALU.add)


def is_step(n):
    return not isinstance(n, int) or 0 <= n < NSTEP


class Banks:

    def __init__(self, i, stages, full, drained):
        self.i, self.stages, self.full, self.drained = i, stages, full, drained
        self.bank = {name: b for _, _, name, b in PIECES}

    def pieces(self, step):
        return [name for s, st, name, _ in PIECES if s == step and st in self.stages]

    def count(self, name):
        b = self.bank[name]
        return uses_before(self.i, b) + uses(b, self.stages, name)

    def wait_free(self, eng, name):
        wait(eng, self.drained[self.bank[name]], self.count(name))

    def wait_full(self, eng, name):
        wait(eng, self.full[self.bank[name]], self.count(name) + 1)

    def is_drained(self, name):
        return self.drained[self.bank[name]], self.count(name) + 1

    def wait_drained(self, eng, name):
        wait(eng, *self.is_drained(name))


class Chain:

    def __init__(self, eng, sem, base):
        self.eng, self.sem, self.base, self.n = eng, sem, base, 0

    def mark(self, ins):
        self.n += 1
        return ins.then_inc(self.sem, 1)

    def sync(self):
        wait(self.eng, *self.last())

    def last(self):
        return self.sem, self.base + self.n


def repeat(ap, n):
    s = list(ap.shape)
    return ap.unsqueeze(1).broadcast_to([s[0], n] + s[1:])


def attention_block(nc, d):
    with ExitStack() as ctx:
        def sb(name, shape, dt):
            return ctx.enter_context(nc.sbuf_tensor(name, shape, dt))

        def sem(name):
            return ctx.enter_context(nc.semaphore(name))

        raw = sb("raw", [P, 2 * 3 * C + 2 * C], F32)
        wtok = sb("wtok", [P, KT, C], F32)
        wa_hi, wa_lo = sb("wa_hi", [P, 2, 3 * C], F32R), sb("wa_lo", [P, 2, 3 * C], F32R)
        wp_hi, wp_lo = sb("wp_hi", [P, 2, C], F32R), sb("wp_lo", [P, 2, C], F32R)
        wg0, wg1 = sb("wg0", [P, E], F32), sb("wg1", [C2, E], F32)
        bqk = sb("bqk", [P, 3], F32)
        bv, bp = sb("bv", [P, C], F32), sb("bp", [P, C], F32)
        postab, biastab = sb("postab", [P, 2, C], F32), sb("biastab", [P, 2, C], F32)
        addend = sb("addend", [P, 2, C], F32)
        selb = sb("selb", [P, 8 * P], BF16)
        sel = sb("sel", [P, 8, P], F32R)
        row2b, row2 = sb("row2b", [2, 2 * P], BF16), sb("row2", [2, 2, P], F32R)
        ident = sb("ident", [P, P], F32)
        masks = sb("masks", [P, 4, P], BF16)
        identb, maskb, onesb, lowb = (masks[:, n, :] for n in range(4))
        iota8, kbase = sb("iota8", [P, E], F32), sb("kbase", [P, 4, K2], F32)
        valid, tid = sb("valid", [P, 4], F32), sb("tid", [P, 4], F32)
        half = sb("half", [P, 4], F32)
        blank = sb("blank", [P, K2, TRIES, ROW], F32)
        zeros = sb("zeros", [P, 7 * C], F32)
        word_v, word_p = sb("word_v", [1, NWORDS], F32), sb("word_p", [1, NWORDS], F32)
        x = [sb(f"x{n}", [P, KT, TP], F32) for n in range(2)]
        h = sb("h", [P, 4, C], F32)
        hb = [sb(f"hb{n}", [P, 4, C], F32) for n in range(2)]
        h0_hi, h0_lo, h1 = (sb(n, [P, TP], F32R) for n in ("h0_hi", "h0_lo", "h1"))
        qk_hi = [sb(f"qk_hi{n}", [P, TP], F32R) for n in range(3)]
        qk_lo = [sb(f"qk_lo{n}", [P, TP], F32R) for n in range(3)]
        qs = [sb(f"qs{n}", [P, NH // 2, TP], F32R) for n in range(2)]
        ks = [sb(f"ks{n}", [P, NH // 2, TP], F32R) for n in range(2)]
        v32, vrest = sb("v32", [P, 4, C], F32), sb("vrest", [P, 4, C], F32)
        h_twice, y_twice = sb("h_twice", [P, 4, P], F32), sb("y_twice", [P, 4, P], F32)
        vs = [sb(f"vs{n}", [P, 4, NH, 3, VW], BF16) for n in range(2)]
        rmax = [sb(f"rmax{n}", [P, 2, 2], F32) for n in range(2)]
        maxrow = [sb(f"maxrow{n}", [2, TI], F32R) for n in range(2)]
        p32 = [sb(f"p32_{n}", [P, 2, TI + T1], F32) for n in range(2)]
        p_hi = [sb(f"p_hi{n}", [P, 2, TI + T1], F16) for n in range(2)]
        p_lo = [sb(f"p_lo{n}", [P, 2, TI + T1], F16) for n in range(2)]
        ys = sb("ys", [P, 2, NH, VW], F32)
        rden = sb("rden", [P, 2, NH], F32)
        y32 = [sb(f"y32_{n}", [P, 4, C], F32) for n in range(2)]
        y0_hi, y0_lo, y1 = (sb(n, [P, TP], F32R) for n in ("y0_hi", "y0_lo", "y1"))
        r = sb("r", [P, 4, C], F32)
        stats, mv = sb("stats", [P, 4, 6], F32), sb("mv", [P, 4, 2], F32)
        rstd = sb("rstd", [P, 4], F32)
        pay = [sb(f"pay{n}", [P, 4, C + 4], F32) for n in range(2)]
        xt0, xt1 = sb("xt0", [P, TP], F32), sb("xt1", [C2, TP], F32)
        logit, top = sb("logit", [P, 4, E], F32), sb("top", [P, 4, E], F32)
        topi = sb("topi", [P, 4, E], U32)
        idf, rank, over, sl = (sb(n, [P, 4, K2], F32) for n in ("idf", "rank", "over", "sl"))
        slot = [sb(f"slot{n}", [P, 4, K2], I32) for n in range(2)]
        oh = sb("oh", [P, 4, K2, E], F32)
        ohb, acc = sb("ohb", [P, 4, K2 * E], BF16), sb("acc", [P, 5, K2 * E], BF16)
        pos, po = sb("pos", [P, 4, K2 * E], F32), sb("po", [P, 4, K2 * E], F32)
        carry = sb("carry", [P, K2 * E], F32)
        dif, ex, den = (sb(n, [P, 4], F32) for n in ("dif", "ex", "den"))

        G = [ctx.enter_context(nc.psum_tensor(f"G{n}", [P, 512], F32)) for n in range(2)]
        PV = ctx.enter_context(nc.psum_tensor("PV", [P, 512], F32))
        MT = ctx.enter_context(nc.psum_tensor("MT", [P, 512], F32))
        S = ctx.enter_context(nc.psum_tensor("S", [P, 2, 512], F32))
        ST = ctx.enter_context(nc.psum_tensor("ST", [P, 2, 512], F32))

        s_w, s_const = sem("weights_loaded"), sem("constants_ready")
        s_whi, s_set = sem("weights_hi"), sem("buffers_set")
        s_blank, s_clear = sem("blank_ready"), sem("dram_cleared")
        full = [sem("general0_full"), sem("general1_full")]
        drained = [sem("general0_drained"), sem("general1_drained")]
        s_x = [sem("x0_loaded"), sem("x1_loaded")]
        s_hi1, s_hi3 = sem("hi_part1"), sem("hi_part3")
        s_htwice, s_ytwice = sem("h_columns_twice"), sem("y_columns_twice")
        s_hb, s_vstep, s_vsplit = sem("h_plus_bias"), sem("v_step"), sem("v_split")
        s_d2, s_d3 = sem("vector_step2"), sem("vector_step3")
        s_s, s_m = sem("scores_full"), sem("max_ready")
        s_mt, s_mrow = sem("max_turned"), sem("max_row_ready")
        s_st, s_exp = sem("turned_scores_full"), sem("exp_ready")
        s_mask, s_phi, s_plo = sem("p_masked"), sem("p_hi_ready"), sem("p_lo_ready")
        s_pv, s_pvt, s_y = sem("pv_full"), sem("pv_taken"), sem("y_ready")
        s_var, s_rstd = sem("variance_ready"), sem("rstd_ready")
        s_dif, s_ex = sem("gate_difference"), sem("gate_exp")
        s_x1, s_slot = sem("x1_ready"), sem("slots_ready")
        s_st1 = [sem("x1_stored0"), sem("x1_stored1")]
        s_sc = [sem("rows_scattered0"), sem("rows_scattered1")]

        loads = [(wtok, "wtok"), (raw, "raw"), (wg0, "wg0"), (wg1, "wg1"), (bqk, "bqk"),
                 (bv, "bv"), (bp, "bp"), (postab, "pos"), (biastab, "bias"), (selb, "sel"),
                 (row2b, "row2"), (ident, "ident"), (masks, "masks"), (iota8, "iota8"),
                 (kbase, "kbase"), (valid, "valid"), (tid, "tid")]
        SETS = 18
        NCLEAR = E * K2 + 5
        READY = 6

        def body_at(i):
            return Banks(i, stages_of(i) if isinstance(i, int) else (1, 2, 3, 4), full, drained)

        block = ctx.enter_context(nc.Block())

        @block.sync
        def _(sp):
            for dst, name in loads:
                sp.dma_start(dst[:], d[name]).then_inc(s_w, 16)

            def body(i, turn, par, stages):
                if 1 in stages:
                    if not isinstance(i, int) or i >= 2:
                        body_at(i - 2).wait_full(sp, "E1")
                    sp.dma_start(x[par][:], d["xt"][i]).then_inc(s_x[par], 16)
                if 3 in stages:
                    p = i - 2
                    sp.wait_ge(s_x1, p + 1)
                    for n, (im, hf, _, _) in enumerate(TILES):
                        sp.dma_start(d["x1"][bass.ds(p * (2 * T) + (im * T + hf * P), REAL[n]), :],
                                     pay[par][0:REAL[n], n, 2:2 + C]).then_inc(s_st1[par], 16)
            run_bodies(sp, body)
            for par in range(2):
                sp.wait_ge(s_st1[par], NPAIR // 2 * 4 * 16)

        @block.gpsimd
        def _(pool):
            for t, value in ((h, 0.0), (v32, 0.0), (logit, 0.0), (r, 0.0), (ys, 1.0), (half, -0.5),
                             (acc, 0.0), (carry, 0.0), (zeros, 0.0), (p32[0], 0.0), (p32[1], 0.0),
                             (pay[0], 0.0), (pay[1], 0.0), (vs[0], 0.0), (vs[1], 0.0), (blank, 0.0),
                             (word_v, 0.0), (word_p, 0.0)):
                pool.memset(t[:], value).then_inc(s_set, 1)
            pool.wait_ge(s_set, SETS)
            words = Words(pool, word_p)
            for n in range(2):
                pool.memset(vs[n][:, :, :, 0, HD:VW], 1.0).then_inc(s_const, 1)
                c = ROW - 1 if n == 0 else 1
                pool.memset(blank[:, n, :, c:c + 1], FAR).then_inc(s_blank, 1)

            def twice(dst, src):
                return pool.tensor_copy(dst[:].rearrange("p t (a b) -> p t a b", a=2),
                                        src[:, :, P:C].unsqueeze(2).broadcast_to([P, 4, 2, C2]))

            def body(i, turn, par, stages):
                g = body_at(i)
                for s in range(STEPS):
                    n = (i - 1) * STEPS + s - 2
                    if s == 2 and 1 in stages:
                        words.wait( g.is_drained("E1"))
                        twice(h_twice, h).then_inc(s_htwice, 1)
                    if s == 4 and 3 in stages:
                        words.wait( (s_y, (i - 1) * 2))
                        twice(y_twice, y32[par]).then_inc(s_ytwice, 1)
                    if (2 in stages or s < 2) and is_step(n):
                        b = s % 2
                        words.wait( (s_exp, n + 1))
                        pool.affine_select(out=p32[b][:, :, 0:P], in_=p32[b][:, :, 0:P],
                                           compare_op=ALU.is_ge, fill=0.0, base=0,
                                           pattern=[[0, 2], [1, P]], channel_multiplier=-1)\
                            .then_inc(s_mask, 1)
                        pool.affine_select(out=p32[b][0:T1, :, TI:TI + T1],
                                           in_=p32[b][0:T1, :, TI:TI + T1],
                                           compare_op=ALU.is_ge, fill=0.0, base=0,
                                           pattern=[[0, 2], [1, T1]], channel_multiplier=-1)\
                            .then_inc(s_mask, 1)
                        words.wait( (s_mask, n * 2 + 2), (s_pv, n - 1))
                        pool.tensor_copy(p_hi[b][:], p32[b][:]).then_inc(s_phi, 1)
                    if s < 8 and 4 in stages:
                        p, o = i - 3, 1 - par
                        t, k = s // 2, s % 2
                        if s == 0:
                            words.wait( (s_clear, 16 * NCLEAR), (s_slot, p + 1))
                        first = 2 if k == 0 else 0
                        pool.indirect_dma_start(
                            d["lists"][:, :],
                            bass.IndirectOffsetOnAxis(ap=slot[o][0:REAL[t], t, k:k + 1], axis=0),
                            pay[o][0:REAL[t], t, first:first + ROW], None,
                            bounds_check=NSLOT - 1, oob_is_err=False).then_inc(s_sc[o], 16)
                    if s == 7 and 3 in stages:
                        pool.wait_ge(s_var, i - 1)
                        pool.tensor_tensor(rstd[:], rstd[:], half[:], ALU.pow).then_inc(s_rstd, 1)
                    if s == 7 and 1 in stages:
                        g.wait_drained(pool, "E1")
                        if 3 in stages:
                            g.wait_drained(pool, "PR1")
                        pool.tensor_tensor(hb[par][:], h[:], repeat(bp[:], 4), ALU.add)\
                            .then_inc(s_hb, 1)
                if 1 in stages:
                    words.wait( g.is_drained("V0"), g.is_drained("V1"))
                    part = [vs[par][:, :, :, c, 0:HD].rearrange("p t h e -> p (t h) e")
                            for c in range(3)]
                    v3 = v32[:].rearrange("p t (h e) -> p (t h) e", e=HD)
                    r3 = vrest[:].rearrange("p t (h e) -> p (t h) e", e=HD)
                    pool.tensor_copy(part[0], v3).then_inc(s_vstep, 1)
                    pool.wait_ge(s_vstep, i * 3 + 1)
                    pool.tensor_tensor(r3, v3, part[0], ALU.subtract).then_inc(s_vstep, 1)
                    words.wait( (s_vstep, i * 3 + 2))
                    pool.tensor_copy(part[1], r3).then_inc(s_vstep, 1)
                    pool.wait_ge(s_vstep, i * 3 + 3)
                    pool.tensor_tensor(part[2], r3, part[1], ALU.subtract).then_inc(s_vsplit, 1)
            run_bodies(pool, body)
            for par in range(2):
                pool.wait_ge(s_sc[par], NPAIR // 2 * 8 * 16)

        @block.scalar
        def _(act):
            act.wait_ge(s_blank, 2)
            act.wait_ge(s_set, SETS)
            for e in range(E):
                for k in range(K2):
                    at = (e * K2 + k) * SEG
                    dst = d["lists"][at:at + SEG, :].rearrange("(p a t) c -> p a (t c)", p=P, t=TRIES)
                    src = blank[:, k].rearrange("p t c -> p (t c)")
                    act.dma_start(dst, repeat(src, SEG // P // TRIES)).then_inc(s_clear, 16)
            yd = d["y"].rearrange("(p t) c -> p (t c)", p=P)
            for q in range(4):
                dst = yd[:, q * 49 * C:(q + 1) * 49 * C].rearrange("p (a c) -> p a c", c=7 * C)
                act.dma_start(dst, repeat(zeros[:], 7)).then_inc(s_clear, 16)
            act.dma_start(yd[:, 196 * C:197 * C], zeros[:, 0:C]).then_inc(s_clear, 16)
            act.wait_ge(s_w, 16 * len(loads))
            act.activation(sel[:].rearrange("p a b -> p (a b)"), selb[:], ACT.Copy).then_inc(s_const, 1)
            act.activation(row2[:].rearrange("p a b -> p (a b)"), row2b[:], ACT.Copy)\
                .then_inc(s_const, 1)
            a = 2 * 3 * C
            act.activation(wa_hi[:].rearrange("p a b -> p (a b)"), raw[:, 0:a], ACT.Copy)\
                .then_inc(s_whi, 1)
            act.activation(wp_hi[:].rearrange("p a b -> p (a b)"), raw[:, a:], ACT.Copy)\
                .then_inc(s_whi, 1)

            def hi_pair(g, name, dst, sem_):
                g.wait_full(act, name)
                act.activation(dst, G[g.bank[name]][:, 0:TP], ACT.Copy).then_inc(sem_, 1)

            def body(i, turn, par, stages):
                g = body_at(i)
                for s in range(STEPS):
                    n = (i - 1) * STEPS + s
                    if (2 in stages or s < 1) and is_step(n - 1):
                        act.wait_ge(s_mt, n)
                        act.activation(maxrow[(s - 1) % 2][:], MT[0:2, 0:TI], ACT.Copy)\
                            .then_inc(s_mrow, 1)
                    if (2 in stages or s < 2) and is_step(n - 2):
                        b = s % 2
                        act.wait_ge(s_st, n - 1)
                        wait(act, s_plo, n - 3)
                        act.activation(p32[b][:, :, 0:TI], ST[:, :, 0:TI], ACT.Exp, scale=SCALE)
                        act.activation(p32[b][0:T1, :, TI:TI + T1], ST[0:T1, :, TI:TI + T1],
                                       ACT.Exp, scale=SCALE).then_inc(s_exp, 1)
                    for name in g.pieces(s):
                        src = G[g.bank[name]]
                        if name == "TX0":
                            hi_pair(g, name, h0_hi[:], s_hi1)
                        elif name == "TX1":
                            hi_pair(g, name, h1[:], s_hi1)
                        elif name == "TY0":
                            hi_pair(g, name, y0_hi[:], s_hi3)
                        elif name == "TY1":
                            hi_pair(g, name, y1[:], s_hi3)
                        elif name[:2] == "QK":
                            t = int(name[2:])
                            g.wait_full(act, name)
                            act.activation(qk_hi[t][:], src[:, 0:TP], ACT.Identity,
                                           bias=bqk[:, t:t + 1]).then_inc(s_hi1, 1)
                        elif name[:2] == "SL" and int(name[2:]) % 2 == 0:
                            g.wait_full(act, name)
                            q = int(name[2:])
                            dst = qs if q % 4 < 2 else ks
                            act.activation(dst[par][:, 2 * (q // 4) + q % 2, :], src[:, 0:TP], ACT.Copy)\
                                .then_inc(drained[g.bank[name]], 1)
                        elif name == "TR0":
                            g.wait_full(act, name)
                            act.activation(xt0[:], src[:, 0:TP], ACT.Copy)\
                                .then_inc(drained[g.bank[name]], 1)
                        elif name == "TR1":
                            g.wait_full(act, name)
                            act.activation(xt1[:], src[0:C2, 0:TP], ACT.Copy)\
                                .then_inc(drained[g.bank[name]], 1)
                        elif name == "RT":
                            act.wait_ge(s_dif, i - 1)
                            act.activation(ex[:], dif[:], ACT.Exp).then_inc(s_ex, 1)
            run_bodies(act, body)
            act.wait_ge(s_clear, 16 * NCLEAR)

        @block.tensor
        def _(pe):
            pe.wait_ge(s_w, 16 * len(loads))
            pe.wait_ge(s_const, READY)

            def turned(g, name, src, first, width=P):
                g.wait_free(pe, name)
                b = g.bank[name]
                for t, (_, _, col, rows) in enumerate(TILES):
                    mm = pe.transpose(G[b][0:width, col:col + rows],
                                      src[0:rows, t, first:first + width], ident[0:rows, 0:rows])
                mm.then_inc(full[b], 1)

            def five(out, lhs, rhs):
                for n in range(5):
                    mm = pe.matmul(out, lhs[n], rhs[n], start=(n == 0), stop=(n == 4))
                return mm

            def body(i, turn, par, stages):
                g = body_at(i)
                pb = 1 - par
                for s in range(STEPS):
                    n = (i - 1) * STEPS + s
                    im, j = s // 6, s % 6
                    c0 = im * TI
                    if 2 in stages:
                        if s == 0:
                            body_at(i - 1).wait_drained(pe, "SL10")
                            body_at(i - 1).wait_drained(pe, "SL11")
                        wait(pe, s_m, n)
                        for hh in range(2):
                            hp = slice(64 * hh, 64 * hh + 64)
                            pe.matmul(S[:, hh, 0:P], qs[pb][hp, j, c0:c0 + P], ks[pb][hp, j, c0:c0 + P],
                                      start=True, stop=False)
                            pe.matmul(S[:, hh, 0:P], identb, maskb, start=False, stop=True)
                            pe.matmul(S[0:T1, hh, P:P + TI], qs[pb][hp, j, c0 + P:c0 + TI],
                                      ks[pb][hp, j, c0:c0 + TI], start=True, stop=False)
                            mm = pe.matmul(S[0:T1, hh, 2 * P:2 * P + T1], identb[0:T1, 0:T1],
                                           maskb[0:T1, 0:T1], start=False, stop=True)
                        mm.then_inc(s_s, 1)
                    if (2 in stages or s < 1) and is_step(n - 1):
                        q = (s - 1) % 2
                        pe.wait_ge(s_m, n)
                        wait(pe, s_mrow, n - 1)
                        pe.transpose(MT[0:2, 0:P], rmax[q][:, 0, :], ident[:])
                        pe.transpose(MT[0:2, P:TI], rmax[q][0:T1, 1, :], ident[0:T1, 0:T1])\
                            .then_inc(s_mt, 1)
                    if (2 in stages or s < 2) and is_step(n - 2):
                        s2 = (s - 2) % STEPS
                        im2, j2 = s2 // 6, s2 % 6
                        cc, b2 = im2 * TI, (pb if s >= 2 else par)
                        row = maxrow[s % 2]
                        pe.wait_ge(s_mrow, n - 1)
                        wait(pe, s_exp, n - 2)
                        for hh in range(2):
                            hp = slice(64 * hh, 64 * hh + 64)
                            pe.matmul(ST[:, hh, 0:TI], ks[b2][hp, j2, cc:cc + P],
                                      qs[b2][hp, j2, cc:cc + TI], start=True, stop=False)
                            pe.matmul(ST[:, hh, 0:TI], row2[:, hh, :], row[:], start=False, stop=True)
                            pe.matmul(ST[0:T1, hh, TI:TI + T1], ks[b2][hp, j2, cc + P:cc + TI],
                                      qs[b2][hp, j2, cc + P:cc + TI], start=True, stop=False)
                            mm = pe.matmul(ST[0:T1, hh, TI:TI + T1], row2[:, hh, 0:T1],
                                           row[:, P:TI], start=False, stop=True)
                        mm.then_inc(s_st, 1)
                    for name in g.pieces(s):
                        b = g.bank[name]
                        if name[0] == "E":
                            if name == "E0":
                                pe.wait_ge(s_x[par], (turn + 1) * 16)
                            g.wait_free(pe, name)
                            for hf in range(2):
                                _, _, col, rows = TILES[2 * int(name[1]) + hf]
                                for k in range(KT):
                                    mm = pe.matmul(G[b][0:rows, hf * C:(hf + 1) * C],
                                                   x[par][:, k, col:col + rows], wtok[:, k, :],
                                                   start=(k == 0), stop=(k == KT - 1))
                            mm.then_inc(full[b], 1)
                        elif name[:2] == "TX":
                            if name == "TX0":
                                g.wait_drained(pe, "E0")
                                g.wait_drained(pe, "E1")
                                turned(g, name, h, 0)
                            else:
                                pe.wait_ge(s_htwice, i + 1)
                                turned(g, name, h_twice, 0)
                        elif name[:2] == "TY":
                            if name == "TY0":
                                pe.wait_ge(s_y, (i - 1) * 2)
                                turned(g, name, y32[par], 0)
                            else:
                                pe.wait_ge(s_ytwice, i - 1)
                                turned(g, name, y_twice, 0)
                        elif name[:2] == "TR":
                            if name == "TR0":
                                pe.wait_ge(s_x1, i - 1)
                                turned(g, name, pay[par], 2)
                            else:
                                turned(g, name, pay[par], 2 + P, C2 + 2)
                        elif name[:2] == "QK":
                            t = int(name[2])
                            if t == 0:
                                g.wait_drained(pe, "TX0")
                                g.wait_drained(pe, "TX1")
                            g.wait_free(pe, name)
                            w = slice(t * P, (t + 1) * P)
                            five(G[b][:, 0:TP],
                                 [wa_hi[:, 0, w], wa_hi[:, 0, w], wa_lo[:, 0, w], wa_hi[:, 1, w],
                                  wa_lo[:, 1, w]],
                                 [h0_hi[:], h0_lo[:], h0_hi[:], h1[:], h1[:]]).then_inc(full[b], 1)
                        elif name[:2] == "SL":
                            q = int(name[2:])
                            t, which, jj = q // 4, (q % 4) // 2, q % 2
                            g.wait_drained(pe, f"QK{t}")
                            g.wait_free(pe, name)
                            for part in range(2):
                                mm = pe.matmul(G[b][:, 0:TP], sel[:, 4 * which + 2 * jj + part, :],
                                               (qk_lo if part else qk_hi)[t][:],
                                               start=(part == 0), stop=(part == 1))
                            mm.then_inc(full[b], 1)
                        elif name[0] == "V":
                            g.wait_free(pe, name)
                            for hf in range(2):
                                _, _, col, rows = TILES[2 * int(name[1]) + hf]
                                c = slice(col, col + rows)
                                w = slice(2 * C, 3 * C)
                                mm = five(G[b][0:rows, hf * C:(hf + 1) * C],
                                          [h0_hi[:, c], h0_lo[:, c], h0_hi[:, c], h1[:, c], h1[:, c]],
                                          [wa_hi[:, 0, w], wa_hi[:, 0, w], wa_lo[:, 0, w],
                                           wa_hi[:, 1, w], wa_lo[:, 1, w]])
                            mm.then_inc(full[b], 1)
                        elif name[:2] == "PR":
                            if name == "PR0":
                                g.wait_drained(pe, "TY0")
                                g.wait_drained(pe, "TY1")
                            g.wait_free(pe, name)
                            for hf in range(2):
                                _, _, col, rows = TILES[2 * int(name[2]) + hf]
                                c = slice(col, col + rows)
                                mm = five(G[b][0:rows, hf * C:(hf + 1) * C],
                                          [y0_hi[:, c], y0_lo[:, c], y0_hi[:, c], y1[:, c], y1[:, c]],
                                          [wp_hi[:, 0], wp_hi[:, 0], wp_lo[:, 0], wp_hi[:, 1],
                                           wp_lo[:, 1]])
                            mm.then_inc(full[b], 1)
                        elif name == "LG":
                            g.wait_drained(pe, "TR0")
                            g.wait_drained(pe, "TR1")
                            g.wait_free(pe, name)
                            for t, (_, _, col, rows) in enumerate(TILES):
                                o = G[b][0:rows, t * E:(t + 1) * E]
                                pe.matmul(o, xt0[:, col:col + rows], wg0[:], start=True, stop=False)
                                mm = pe.matmul(o, xt1[:, col:col + rows], wg1[:], start=False, stop=True)
                            mm.then_inc(full[b], 1)
                        elif name == "RT":
                            pe.wait_ge(s_dif, i - 1)
                            g.wait_free(pe, name)
                            w = 4 * K2 * E
                            pe.matmul(G[b][:, 0:w], onesb, acc[:, 0:4].rearrange("p a b -> p (a b)"),
                                      start=True, stop=False)
                            pe.matmul(G[b][:, 0:w], lowb, ohb[:].rearrange("p a b -> p (a b)"),
                                      start=False, stop=True)
                            pe.matmul(G[b][:, w:w + K2 * E], onesb, acc[:, 4], start=True, stop=True)\
                                .then_inc(full[b], 1)
                    if (2 in stages or s < 3) and is_step(n - 3):
                        s3 = (s - 3) % STEPS
                        im3, j3 = s3 // 6, s3 % 6
                        b3, q = (pb if s >= 3 else par), (s - 3) % 2
                        pe.wait_ge(s_plo, n - 2)
                        wait(pe, s_pvt, n - 3)
                        if s3 == 0:
                            pe.wait_ge(s_vsplit, i - (0 if s >= 3 else 1))
                        for hh in range(2):
                            hd = 2 * j3 + hh
                            v0 = vs[b3][:, 2 * im3, hd].rearrange("p a b -> p (a b)")
                            v1 = vs[b3][0:T1, 2 * im3 + 1, hd].rearrange("p a b -> p (a b)")
                            o0 = PV[:, hh * 3 * VW:(hh + 1) * 3 * VW]
                            o1 = PV[0:T1, P + hh * 3 * VW:P + (hh + 1) * 3 * VW]
                            pe.matmul(o0, p_hi[q][:, hh, 0:P], v0, start=True, stop=False)
                            pe.matmul(o0, p_lo[q][:, hh, 0:P], v0, start=False, stop=True)
                            pe.matmul(o1, p_hi[q][:, hh, P:TI], v0, start=True, stop=False)
                            pe.matmul(o1, p_lo[q][:, hh, P:TI], v0, start=False, stop=False)
                            pe.matmul(o1, p_hi[q][0:T1, hh, TI:TI + T1], v1, start=False, stop=False)
                            mm = pe.matmul(o1, p_lo[q][0:T1, hh, TI:TI + T1], v1, start=False, stop=True)
                        mm.then_inc(s_pv, 1)
            run_bodies(pe, body)

        @block.vector
        def _(dve):
            dve.wait_ge(s_w, 16 * len(loads))
            dve.tensor_tensor(addend[:], postab[:], biastab[:], ALU.add).then_inc(s_const, 1)
            dve.wait_ge(s_whi, 2)
            a = 2 * 3 * C
            dve.tensor_tensor(wa_lo[:].rearrange("p a b -> p (a b)"), raw[:, 0:a],
                              wa_hi[:].rearrange("p a b -> p (a b)").bitcast(F32), ALU.subtract)
            dve.tensor_tensor(wp_lo[:].rearrange("p a b -> p (a b)"), raw[:, a:],
                              wp_hi[:].rearrange("p a b -> p (a b)").bitcast(F32), ALU.subtract)\
                .then_inc(s_const, 1)
            dve.wait_ge(s_set, SETS)
            dve.wait_ge(s_const, READY)
            words = Words(dve, word_v)
            D3 = 23

            def rest(src, hi, lo, rows):
                return dve.tensor_tensor(lo[rows], src[rows, 0:TP], hi[rows].bitcast(F32), ALU.subtract)

            def body(i, turn, par, stages):
                g = body_at(i)
                every, upper = slice(0, P), slice(C2, P)
                p = i - 2
                ch = Chain(dve, s_d3, p * D3)
                pb = pay[par]
                for s in range(STEPS):
                    n = (i - 1) * STEPS + s
                    if 2 in stages:
                        dve.wait_ge(s_s, n + 1)
                        wait(dve, s_mt, n - 1)
                        q = s % 2
                        dve.tensor_reduce(rmax[q][:, 0, :], S[:, :, 0:P], AX.X, ALU.max, negate=True)
                        dve.tensor_reduce(rmax[q][0:T1, 1, :], S[0:T1, :, P:P + TI], AX.X, ALU.max,
                                          negate=True).then_inc(s_m, 1)
                    for name in g.pieces(s):
                        b = g.bank[name]
                        src = G[b]
                        if name[0] == "E":
                            g.wait_full(dve, name)
                            if name == "E0":
                                wait(dve, s_hb, i)
                            for hf in range(2):
                                t = 2 * int(name[1]) + hf
                                rows = TILES[t][3]
                                ins = dve.scalar_tensor_tensor(
                                    out=h[0:rows, t, :], in0=src[0:rows, hf * C:(hf + 1) * C],
                                    scalar=1.0 / 255.0, in1=addend[0:rows, hf, :],
                                    op0=ALU.mult, op1=ALU.add)
                            ins.then_inc(drained[b], 1)
                        elif name in ("TX0", "TX1", "TY0", "TY1"):
                            k = int(name[2])
                            if name[1] == "X":
                                dve.wait_ge(s_hi1, i * 5 + (k + 1))
                                hi, lo = (h0_hi, h0_lo) if k == 0 else (h1, h1)
                            else:
                                dve.wait_ge(s_hi3, p * 2 + (k + 1))
                                hi, lo = (y0_hi, y0_lo) if k == 0 else (y1, y1)
                            rest(src, hi, lo, every if k == 0 else upper).then_inc(drained[b], 1)
                        elif name[:2] == "QK":
                            t = int(name[2])
                            dve.wait_ge(s_hi1, i * 5 + (t + 3))
                            dve.scalar_tensor_tensor(
                                out=qk_lo[t][:], in0=src[:, 0:TP], scalar=bqk[:, t:t + 1],
                                in1=qk_hi[t][:].bitcast(F32), op0=ALU.add, op1=ALU.subtract)\
                                .then_inc(drained[b], 1)
                        elif name[:2] == "SL" and int(name[2:]) % 2 == 1:
                            g.wait_full(dve, name)
                            q = int(name[2:])
                            dst = qs if q % 4 < 2 else ks
                            dve.tensor_copy(dst[par][:, 2 * (q // 4) + q % 2, :], src[:, 0:TP])\
                                .then_inc(drained[b], 1)
                        elif name[0] == "V":
                            g.wait_full(dve, name)
                            wait(dve, s_vsplit, i)
                            for hf in range(2):
                                t = 2 * int(name[1]) + hf
                                rows = TILES[t][3]
                                ins = dve.tensor_tensor(v32[0:rows, t, :],
                                                        src[0:rows, hf * C:(hf + 1) * C],
                                                        bv[0:rows, :], ALU.add)
                            ins.then_inc(drained[b], 1)
                        elif name[:2] == "PR":
                            g.wait_full(dve, name)
                            wait(dve, s_hb, i - 1)
                            for hf in range(2):
                                t = 2 * int(name[2]) + hf
                                rows = TILES[t][3]
                                ins = dve.tensor_tensor(r[0:rows, t, :],
                                                        src[0:rows, hf * C:(hf + 1) * C],
                                                        hb[par][0:rows, t, :], ALU.add)
                            ins.then_inc(drained[b], 1)
                            if name == "PR1":
                                g.wait_drained(dve, "PR0")
                                g.wait_drained(dve, "PR1")
                                for t in range(4):
                                    ins = dve.bn_stats(stats[:, t, :], r[:, t, :])
                                ch.mark(ins)
                                words.wait( ch.last())
                                for t in range(4):
                                    ins = dve.bn_aggr(mv[:, t, :], stats[:, t, :])
                                ch.mark(ins)
                                ch.sync()
                                dve.tensor_scalar(rstd[:], mv[:, :, 1], EPS, None, ALU.add)\
                                    .then_inc(s_var, 1)
                        elif name == "LG":
                            g.wait_full(dve, name)
                            lv = src[:, 0:4 * E].rearrange("p (a b e) -> p a b e", b=2, e=E)
                            dst = logit[:].rearrange("p (a b) e -> p a b e", b=2)
                            dve.tensor_copy(dst[:, :, 0], lv[:, :, 0])
                            dve.tensor_copy(dst[0:T1, :, 1], lv[0:T1, :, 1]).then_inc(drained[b], 1)
                            words.wait( g.is_drained("LG"))
                            for t in range(4):
                                ins = dve.max(top[:, t, :], logit[:, t, :])
                            ch.mark(ins)
                            words.wait( ch.last())
                            for t in range(4):
                                ins = dve.max_index(topi[:, t, :], top[:, t, :], logit[:, t, :])
                            ch.mark(ins)
                            ch.sync()
                            ch.mark(dve.tensor_copy(idf[:], topi[:, :, 0:K2]))
                            ch.sync()
                            ch.mark(dve.tensor_tensor(
                                oh[:], iota8[:].unsqueeze(1).unsqueeze(1).broadcast_to([P, 4, K2, E]),
                                idf[:].unsqueeze(3).broadcast_to([P, 4, K2, E]), ALU.is_equal))
                            ch.sync()
                            ch.mark(dve.tensor_tensor(
                                ohb[:], oh[:].rearrange("p a b c -> p a (b c)"),
                                valid[:].unsqueeze(2).broadcast_to([P, 4, K2 * E]), ALU.mult))
                            ch.sync()
                            for t in range(4):
                                ch.mark(dve.tensor_tensor(acc[:, t + 1], acc[:, t], ohb[:, t], ALU.add))
                                ch.sync()
                            dve.tensor_tensor(dif[:], top[:, :, 1], top[:, :, 0], ALU.subtract)\
                                .then_inc(s_dif, 1)
                        elif name == "RT":
                            g.wait_full(dve, name)
                            w = 4 * K2 * E
                            ch.mark(dve.tensor_tensor(
                                pos[:], src[:, 0:w].rearrange("p (a b) -> p a b", a=4),
                                repeat(carry[:], 4), ALU.add))
                            ch.sync()
                            dve.tensor_tensor(carry[:], src[:, w:w + K2 * E], carry[:], ALU.add)\
                                .then_inc(drained[b], 1)
                            ch.mark(dve.tensor_tensor(po[:], pos[:], ohb[:], ALU.mult))
                            ch.sync()
                            ch.mark(dve.tensor_reduce(
                                rank[:], po[:].rearrange("p a (b c) -> p a b c", b=K2), AX.X, ALU.add))
                            ch.mark(dve.scalar_tensor_tensor(
                                out=sl[:], in0=idf[:], scalar=float(K2 * SEG), in1=kbase[:],
                                op0=ALU.mult, op1=ALU.add))
                            ch.sync()
                            ch.mark(dve.tensor_scalar(over[:], rank[:], float(CAP), FAR,
                                                      ALU.is_ge, ALU.mult))
                            ch.mark(dve.tensor_tensor(sl[:], sl[:], rank[:], ALU.add))
                            ch.sync()
                            ch.mark(dve.tensor_tensor(slot[par][:], sl[:], over[:], ALU.add))
                            dve.wait_ge(s_ex, p + 1)
                            ch.mark(dve.tensor_scalar(den[:], ex[:], 1.0, None, ALU.add))
                            ch.sync()
                            ch.mark(dve.reciprocal(pb[:, :, C + 2], den[:]))
                            ch.mark(dve.tensor_copy(pb[:, :, C + 3], tid[:]))
                            ch.mark(dve.tensor_scalar(pb[:, :, 1], tid[:], float(N), None, ALU.add))
                            ch.sync()
                            ch.mark(dve.tensor_scalar(tid[:], tid[:], float(2 * T), None, ALU.add))
                            dve.tensor_tensor(pb[:, :, 0], ex[:], pb[:, :, C + 2], ALU.mult)\
                                .then_inc(s_slot, 1)
                            assert ch.n == D3, ch.n
                    if s == 7 and 3 in stages:
                        if not isinstance(i, int) or p >= 2:
                            dve.wait_ge(s_st1[par], (turn - 1) * 4 * 16)
                            dve.wait_ge(s_sc[par], (turn - 1) * 8 * 16)
                        dve.wait_ge(s_rstd, p + 1)
                        for t in range(4):
                            ins = dve.tensor_scalar(pb[:, t, 2:2 + C], r[:, t, :], mv[:, t, 0:1],
                                                    rstd[:, t:t + 1], ALU.subtract, ALU.mult)
                        ins.then_inc(s_x1, 1)
                    if (2 in stages or s < 2) and is_step(n - 2):
                        q = s % 2
                        dve.wait_ge(s_phi, n - 1)
                        dve.tensor_tensor(p_lo[q][:], p32[q][:], p_hi[q][:], ALU.subtract)\
                            .then_inc(s_plo, 1)
                    if (2 in stages or s < 3) and is_step(n - 3):
                        s3 = (s - 3) % STEPS
                        im3, j3 = s3 // 6, s3 % 6
                        dve.wait_ge(s_pv, n - 2)
                        if j3 == 0:
                            wait(dve, s_y, (i - 1 if s >= 3 else i - 2) * 2 + im3)
                        for hf, rows in ((0, P), (1, T1)):
                            v = PV[0:rows, hf * P:hf * P + 6 * VW]\
                                .rearrange("p (h c d) -> p h d c", h=2, c=3)
                            ins = dve.tensor_reduce(ys[0:rows, hf, 2 * j3:2 * j3 + 2, :], v, AX.X, ALU.add)
                        ins.then_inc(s_pvt, 1)
                        if j3 == 5:
                            y = y32[1 - par if s >= 3 else par]
                            dve.wait_ge(s_pvt, n - 2)
                            done = (i - 1 if s >= 3 else i - 2) * 2 + (im3 + 1)
                            dve.reciprocal(rden[:], ys[:, :, :, HD]).then_inc(s_d2, 1)
                            dve.wait_ge(s_d2, done)
                            for hf in range(2):
                                ins = dve.tensor_tensor(
                                    y[:, 2 * im3 + hf, :].rearrange("p (h e) -> p h e", e=HD),
                                    ys[:, hf, :, 0:HD],
                                    rden[:, hf].unsqueeze(2).broadcast_to([P, NH, HD]), ALU.mult)
                            ins.then_inc(s_y, 1)
            run_bodies(dve, body)



def expert_block(nc, d):
    CPE = K2 * SEG // TILE3
    NC2 = 2 * CPE
    W1C = 2 * 2 * HID
    with ExitStack() as ctx:
        def sb(name, shape, dt):
            return ctx.enter_context(nc.sbuf_tensor(name, shape, dt))

        def sem(name):
            return ctx.enter_context(nc.semaphore(name))

        ident = sb("e_ident", [P, P], F32)
        word_p = sb("e_word", [1, NWORDS], F32)
        raw = [sb(f"e_raw{n}", [P, WCOLS], F32) for n in range(2)]
        w1_hi = [sb(f"w1_hi{n}", [P, 2, 2 * HID], F32R) for n in range(2)]
        w1_lo = [sb(f"w1_lo{n}", [P, 2, 2 * HID], F32R) for n in range(2)]
        w2 = [sb(f"w2_{n}", [P, HM, 2, C], F32R) for n in range(2)]
        rows = [sb(f"rows{n}", [P, 3, ROW], F32) for n in range(2)]
        twice = [sb(f"twice{n}", [P, 3, P], F32) for n in range(2)]
        wt = [sb(f"wt{n}", [P, 3], F32) for n in range(4)]
        target = [sb(f"target{n}", [P, 3], I32) for n in range(4)]
        x0_hi = [sb(f"ex0_hi{n}", [P, TILE3], F32R) for n in range(2)]
        x0_lo = [sb(f"ex0_lo{n}", [P, TILE3], F32R) for n in range(2)]
        x1 = [sb(f"ex1_{n}", [P, TILE3], F32R) for n in range(2)]
        gate = [sb(f"gate{n}", [P, TILE3], F32) for n in range(2)]
        a32 = [sb(f"a32_{n}", [P, TILE3], F32) for n in range(2)]
        a_hi = [sb(f"a_hi{n}", [P, HM, TILE3], F32R) for n in range(2)]
        a_lo = [sb(f"a_lo{n}", [P, HM, TILE3], F32R) for n in range(2)]
        ylo = [sb(f"ylo{n}", [P, C], F32) for n in range(2)]
        yout = [sb(f"yout{n}", [P, C], F32) for n in range(6)]

        XT = [ctx.enter_context(nc.psum_tensor(f"XT{n}", [P, 512], F32)) for n in range(2)]
        UP = [ctx.enter_context(nc.psum_tensor(f"UP{n}", [P, 512], F32)) for n in range(2)]
        GT = [ctx.enter_context(nc.psum_tensor(f"GT{n}", [P, 512], F32)) for n in range(2)]
        Y = [ctx.enter_context(nc.psum_tensor(f"Y{n}", [P, 512], F32)) for n in range(2)]

        s_id, s_word = sem("e_ident_loaded"), sem("e_word_set")
        s_raw = [sem("weights0_loaded"), sem("weights1_loaded")]
        s_whi, s_wlo = sem("e_weights_hi"), sem("e_weights_split")
        s_rows = [sem("rows0_loaded"), sem("rows1_loaded")]
        s_twice = sem("columns_twice")
        s_xt, s_xhi, s_split = sem("rows_turned"), sem("rows_hi"), sem("rows_split")
        s_ug, s_gate, s_a = sem("hidden_full"), sem("gate_ready"), sem("hidden_ready")
        s_ahi, s_alo = sem("hidden_hi"), sem("hidden_split")
        s_y, s_ylo, s_yout = sem("y_full"), sem("y_lo_scaled"), sem("y_out_ready")
        s_out = [sem(f"y_scattered{n}") for n in range(6)]

        def layout(cc):
            return (0, C, C + 1) if cc % CPE < CPE // 2 else (2, 0, 1)

        def weight_piece(j):
            if j < 8:
                w = W1C // 8
                return slice(j * w, (j + 1) * w), (j // 4, slice(j % 4 * w, (j % 4 + 1) * w))
            m = (j - 8) * (HM // 2)
            return slice(W1C + m * C, W1C + (m + HM // 2) * C), slice(m, m + HM // 2)

        def parts(j, e):
            cols, to = weight_piece(j)
            src = raw[e][:, cols]
            if j < 8:
                return src, w1_hi[e][:, to[0], to[1]], w1_lo[e][:, to[0], to[1]]
            return src.rearrange("p (m c) -> p m c", c=C), w2[e][:, to, 0, :], w2[e][:, to, 1, :]

        block = ctx.enter_context(nc.Block())

        @block.sync
        def _(sp):
            sp.dma_start(ident[:], d["ident"]).then_inc(s_id, 16)
            for e in range(2):
                sp.dma_start(raw[e][:], d["wexp"][e]).then_inc(s_raw[e], 16)
            chunk_rows = d["lists"].rearrange("(n p t) c -> n p t c", p=P, t=3)
            with sp.Fori(0, E // 2) as it:
                for cc in range(NC2):
                    if cc < 2:
                        sp.wait_ge(s_split, it * NC2 + cc if cc else it * NC2)
                    else:
                        sp.wait_ge(s_split, it * NC2 + (cc - 1))
                    sp.dma_start(rows[cc % 2][:], chunk_rows[it * NC2 + cc])\
                        .then_inc(s_rows[cc % 2], 16)
                    if cc % CPE == 2:
                        e = cc // CPE
                        sp.wait_ge(s_wlo, it * 20 + 10 * (e + 1))
                        sp.dma_start(raw[e][:], d["wexp"][it * 2 + (e + 2)]).then_inc(s_raw[e], 16)

        @block.gpsimd
        def _(pool):
            pool.memset(word_p[:], 0.0).then_inc(s_word, 1)
            pool.wait_ge(s_word, 1)
            words = Words(pool, word_p)
            pool.wait_ge(s_raw[0], 16)
            for j in range(10):
                src, hi, _ = parts(j, 0)
                pool.tensor_copy(hi, src).then_inc(s_whi, 1)

            def scatter(it, cc, t):
                n = 3 * cc + t
                words.wait( (s_yout, it * (3 * NC2) + (n + 1)))
                q = 3 * (cc % 2) + t
                pool.indirect_dma_start(
                    d["y"][:, :], bass.IndirectOffsetOnAxis(ap=target[cc % 4][:, t:t + 1], axis=0),
                    yout[q][:], None, bounds_check=K2 * N - 1, oob_is_err=False)\
                    .then_inc(s_out[q], 16)

            def columns_twice(it, cc):
                q, (x0, _, _) = cc % 2, layout(cc)
                words.wait( (s_rows[q], it * (NC2 // 2 * 16) + 16 * (cc // 2 + 1)),
                      (s_xt, it * NC2 + max(cc - 1, 0)))
                pool.tensor_copy(twice[q][:].rearrange("p t (a b) -> p t a b", a=2),
                                 rows[q][:, :, x0 + P:x0 + C].unsqueeze(2).broadcast_to([P, 3, 2, C2]))\
                    .then_inc(s_twice, 1)

            with pool.Fori(0, E // 2) as it:
                columns_twice(it, 0)
                for cc in range(NC2):
                    if cc + 1 < NC2:
                        columns_twice(it, cc + 1)
                    e, j = 1 - cc // CPE, cc % CPE
                    if j == 0:
                        pool.wait_ge(s_raw[e], (it + (1 if e else 2)) * 16)
                    words.wait( (s_ug, it * (4 * NC2) + 4 * cc))
                    src, hi, _ = parts(j, e)
                    pool.tensor_copy(hi, src).then_inc(s_whi, 1)
                    if cc:
                        for t in range(3):
                            scatter(it, cc - 1, t)
                for t in range(3):
                    scatter(it, NC2 - 1, t)
            for q in range(6):
                pool.wait_ge(s_out[q], 16 * (E // 2) * (NC2 // 2))

        @block.tensor
        def _(pe):
            pe.wait_ge(s_id, 16)

            def turn_rows(it, cc):
                x0, _, _ = layout(cc)
                pe.wait_ge(s_rows[cc % 2], it * (NC2 // 2 * 16) + 16 * (cc // 2 + 1))
                for t in range(3):
                    pe.transpose(XT[0][:, t * P:(t + 1) * P], rows[cc % 2][:, t, x0:x0 + P], ident[:])
                pe.wait_ge(s_twice, it * NC2 + (cc + 1))
                for t in range(3):
                    mm = pe.transpose(XT[1][:, t * P:(t + 1) * P], twice[cc % 2][:, t, :], ident[:])
                mm.then_inc(s_xt, 1)

            def first(it, cc, m):
                n, q, e = 4 * cc + m, cc % 2, cc // CPE
                if m == 0:
                    pe.wait_ge(s_split, it * NC2 + (cc + 1))
                    if cc % CPE == 0:
                        pe.wait_ge(s_wlo, it * 20 + 10 * (e + 1))
                if n < 2:
                    pe.wait_ge(s_a, it * (4 * NC2))
                else:
                    pe.wait_ge(s_a, it * (4 * NC2) + (n - 1))
                for bank, c in ((GT[m % 2], HID + m * P), (UP[m % 2], m * P)):
                    w = slice(c, c + P)
                    for k, (a, b) in enumerate(((w1_hi[e][:, 0, w], x0_hi[q]), (w1_hi[e][:, 0, w], x0_lo[q]),
                                                (w1_lo[e][:, 0, w], x0_hi[q]), (w1_hi[e][:, 1, w], x1[q]),
                                                (w1_lo[e][:, 1, w], x1[q]))):
                        mm = pe.matmul(bank[:, 0:TILE3], a, b[:], start=(k == 0), stop=(k == 4))
                mm.then_inc(s_ug, 1)

            def second(it, cc, t):
                n, q, e = 3 * cc + t, cc % 2, cc // CPE
                if t == 0:
                    pe.wait_ge(s_alo, it * (4 * NC2) + 4 * (cc + 1))
                if n < 2:
                    pe.wait_ge(s_yout, it * (3 * NC2))
                else:
                    pe.wait_ge(s_yout, it * (3 * NC2) + (n - 1))
                c = slice(t * P, (t + 1) * P)
                y = Y[n % 2]
                for m in range(HM):
                    def wide():
                        return pe.matmul(y[:, 0:2 * C], a_hi[q][:, m, c],
                                         w2[e][:, m].rearrange("p a b -> p (a b)"),
                                         start=(m == 0), stop=(m == HM - 1))

                    if m < HM - 1:
                        wide()
                    pe.matmul(y[:, 0:C], a_lo[q][:, m, c], w2[e][:, m, 0], start=False, stop=False)
                    if m == HM - 1:
                        mm = wide()
                mm.then_inc(s_y, 1)

            with pe.Fori(0, E // 2) as it:
                turn_rows(it, 0)
                for cc in range(NC2):
                    for m in range(HM):
                        first(it, cc, m)
                        if cc and m < 3:
                            second(it, cc - 1, m)
                        if m == 1 and cc + 1 < NC2:
                            turn_rows(it, cc + 1)
                for t in range(3):
                    second(it, NC2 - 1, t)

        @block.scalar
        def _(act):
            def rows_hi(it, cc):
                act.wait_ge(s_xt, it * NC2 + (cc + 1))
                act.activation(x0_hi[cc % 2][:], XT[0][:, 0:TILE3], ACT.Copy).then_inc(s_xhi, 1)
                act.activation(x1[cc % 2][:], XT[1][:, 0:TILE3], ACT.Copy).then_inc(s_xhi, 1)

            def y_lo(it, cc, t):
                n = 3 * cc + t
                act.wait_ge(s_y, it * (3 * NC2) + (n + 1))
                act.activation(ylo[n % 2][:], Y[n % 2][:, C:2 * C], ACT.Copy,
                               scale=wt[cc % 4][:, t:t + 1]).then_inc(s_ylo, 1)

            def hidden_hi(it, cc, m):
                act.wait_ge(s_a, it * (4 * NC2) + (4 * cc + m + 1))
                act.activation(a_hi[cc % 2][:, m], a32[m % 2][:], ACT.Copy).then_inc(s_ahi, 1)

            with act.Fori(0, E // 2) as it:
                rows_hi(it, 0)
                for cc in range(NC2):
                    for m in range(HM):
                        act.wait_ge(s_ug, it * (4 * NC2) + (4 * cc + m + 1))
                        act.activation(gate[m % 2][:], GT[m % 2][:, 0:TILE3], ACT.Silu).then_inc(s_gate, 1)
                        if cc and m < 3:
                            y_lo(it, cc - 1, m)
                        if m:
                            hidden_hi(it, cc, m - 1)
                        if m == 1 and cc + 1 < NC2:
                            rows_hi(it, cc + 1)
                    hidden_hi(it, cc, HM - 1)
                for t in range(3):
                    y_lo(it, NC2 - 1, t)

        @block.vector
        def _(dve):
            def split_piece(k, j, e):
                dve.wait_ge(s_whi, k)
                src, hi, lo = parts(j, e)
                dve.tensor_tensor(lo, src, hi.bitcast(F32), ALU.subtract).then_inc(s_wlo, 1)

            for j in range(10):
                split_piece(j + 1, j, 0)

            def rows_lo(it, cc):
                q, (x0, w, to) = cc % 2, layout(cc)
                dve.wait_ge(s_rows[q], it * (NC2 // 2 * 16) + 16 * (cc // 2 + 1))
                if cc >= 4:
                    for t in range(3):
                        dve.wait_ge(s_out[3 * q + t], it * (NC2 // 2 * 16) + 16 * (cc // 2 - 1))
                else:
                    for t in range(3):
                        dve.wait_ge(s_out[3 * q + t], it * (NC2 // 2 * 16))
                dve.tensor_copy(wt[cc % 4][:], rows[q][:, :, w])
                dve.tensor_copy(target[cc % 4][:], rows[q][:, :, to])
                dve.wait_ge(s_xhi, it * (2 * NC2) + (2 * cc + 2))
                dve.tensor_tensor(x0_lo[q][:], XT[0][:, 0:TILE3], x0_hi[q][:].bitcast(F32), ALU.subtract)
                dve.tensor_tensor(x1[q][C2:P, :], XT[1][C2:P, 0:TILE3], x1[q][C2:P, :].bitcast(F32),
                                  ALU.subtract).then_inc(s_split, 1)

            def y_out(it, cc, t):
                n, q = 3 * cc + t, 3 * (cc % 2) + t
                dve.wait_ge(s_ylo, it * (3 * NC2) + (n + 1))
                dve.wait_ge(s_out[q], it * (NC2 // 2 * 16) + 16 * (cc // 2)) if cc >= 2 else \
                    dve.wait_ge(s_out[q], it * (NC2 // 2 * 16))
                dve.scalar_tensor_tensor(out=yout[q][:], in0=Y[n % 2][:, 0:C], scalar=wt[cc % 4][:, t:t + 1],
                                         in1=ylo[n % 2][:], op0=ALU.mult, op1=ALU.add).then_inc(s_yout, 1)

            def hidden_lo(it, cc, m):
                dve.wait_ge(s_ahi, it * (4 * NC2) + (4 * cc + m + 1))
                dve.tensor_tensor(a_lo[cc % 2][:, m], a32[m % 2][:], a_hi[cc % 2][:, m].bitcast(F32),
                                  ALU.subtract).then_inc(s_alo, 1)

            with dve.Fori(0, E // 2) as it:
                rows_lo(it, 0)
                for cc in range(NC2):
                    for m in range(HM):
                        dve.wait_ge(s_alo, it * (4 * NC2) + max(4 * cc + m - 1, 0))
                        dve.wait_ge(s_gate, it * (4 * NC2) + (4 * cc + m + 1))
                        dve.tensor_tensor(a32[m % 2][:], UP[m % 2][:, 0:TILE3], gate[m % 2][:], ALU.mult)\
                            .then_inc(s_a, 1)
                        if cc and m < 3:
                            y_out(it, cc - 1, m)
                        if m:
                            hidden_lo(it, cc, m - 1)
                        if m == 1 and cc + 1 < NC2:
                            rows_lo(it, cc + 1)
                    split_piece(it * 20 + (10 + cc + 1), cc % CPE, 1 - cc // CPE)
                    hidden_lo(it, cc, HM - 1)
                for t in range(3):
                    y_out(it, NC2 - 1, t)


def last_block(nc, d, out):
    TPP = 7
    NCH = N // (P * TPP)
    REST = N - NCH * P * TPP
    with ExitStack() as ctx:
        def sb(name, shape, dt):
            return ctx.enter_context(nc.sbuf_tensor(name, shape, dt))

        def sem(name):
            return ctx.enter_context(nc.semaphore(name))

        a = [sb(f"t_x{n}", [P, TPP, C], F32) for n in range(2)]
        y0 = [sb(f"t_y0_{n}", [P, TPP, C], F32) for n in range(2)]
        y1 = [sb(f"t_y1_{n}", [P, TPP, C], F32) for n in range(2)]
        o = [sb(f"t_o{n}", [P, TPP, C], F32) for n in range(2)]
        stats = [sb(f"t_stats{n}", [P, TPP, 6], F32) for n in range(2)]
        mv = [sb(f"t_mv{n}", [P, TPP, 2], F32) for n in range(2)]
        rstd = [sb(f"t_rstd{n}", [P, TPP], F32) for n in range(2)]
        half = sb("t_half", [P, TPP], F32)
        word_v = sb("t_word", [1, NWORDS], F32)
        s_in = [sem("t_loaded0"), sem("t_loaded1")]
        s_half, s_sum, s_all = sem("t_half_ready"), sem("first_sum"), sem("sum_ready")
        s_stat, s_mv, s_var, s_rstd = sem("t_stats"), sem("t_mean"), sem("t_variance"), sem("t_rstd")
        s_o = sem("t_out_ready")
        s_st = [sem("t_stored0"), sem("t_stored1")]
        block = ctx.enter_context(nc.Block())

        def views(ap, first):
            return ap[first:first + NCH * P * TPP, :].rearrange("(n p t) c -> n p t c", p=P, t=TPP)

        x_v, y0_v, y1_v, out_v = (views(ap, f) for ap, f in
                                  ((d["x1"], 0), (d["y"], 0), (d["y"], N), (out, 0)))

        def chunks(eng, body):
            for c in range(2):
                body(c, c // 2, c % 2, P, TPP)
            with eng.Fori(1, NCH // 2) as it:
                for par in range(2):
                    body(it * 2 + par, it, par, P, TPP)
            body(NCH, NCH // 2, 0, REST, 1)

        @block.sync
        def _(sp):
            def body(c, turn, par, rows, t):
                wait(sp, s_o, c - 1)
                for dst, v, ap, f in ((a, x_v, d["x1"], 0), (y0, y0_v, d["y"], 0), (y1, y1_v, d["y"], N)):
                    src = v[c] if rows == P else ap[f + N - REST:f + N, :].unsqueeze(1)
                    sp.dma_start(dst[par][0:rows, 0:t, :], src).then_inc(s_in[par], 16)
            chunks(sp, body)

        @block.gpsimd
        def _(pool):
            pool.memset(half[:], -0.5).then_inc(s_half, 1)
            pool.memset(word_v[:], 0.0).then_inc(s_half, 1)
            pool.wait_ge(s_half, 2)

            def body(c, turn, par, rows, t):
                pool.wait_ge(s_in[par], (turn + 1) * 48)
                pool.tensor_tensor(a[par][0:rows, 0:t], a[par][0:rows, 0:t], y0[par][0:rows, 0:t],
                                   ALU.add).then_inc(s_sum, 1)
                if not isinstance(c, int) or c:
                    power(c - 1, 1 - par, P, TPP)

            def power(c, par, rows, t):
                pool.wait_ge(s_var, c + 1)
                pool.tensor_tensor(rstd[par][0:rows, 0:t], rstd[par][0:rows, 0:t], half[0:rows, 0:t],
                                   ALU.pow).then_inc(s_rstd, 1)
            chunks(pool, body)
            power(NCH, 0, REST, 1)

        @block.vector
        def _(dve):
            words = Words(dve, word_v)

            def finish(c, turn, par, rows, t):
                dve.wait_ge(s_rstd, c + 1)
                wait(dve, s_st[par], turn * 16)
                for n in range(t):
                    ins = dve.tensor_scalar(o[par][0:rows, n, :], a[par][0:rows, n, :],
                                            mv[par][0:rows, n, 0:1], rstd[par][0:rows, n:n + 1],
                                            ALU.subtract, ALU.mult)
                ins.then_inc(s_o, 1)

            def body(c, turn, par, rows, t):
                if isinstance(c, int) and c == 0:
                    dve.wait_ge(s_half, 2)
                dve.wait_ge(s_sum, c + 1)
                dve.tensor_tensor(a[par][0:rows, 0:t], a[par][0:rows, 0:t], y1[par][0:rows, 0:t],
                                  ALU.add).then_inc(s_all, 1)
                dve.wait_ge(s_all, c + 1)
                for n in range(t):
                    ins = dve.bn_stats(stats[par][0:rows, n, :], a[par][0:rows, n, :])
                ins.then_inc(s_stat, 1)
                words.wait( (s_stat, c + 1))
                for n in range(t):
                    ins = dve.bn_aggr(mv[par][0:rows, n, :], stats[par][0:rows, n, :])
                ins.then_inc(s_mv, 1)
                dve.wait_ge(s_mv, c + 1)
                dve.tensor_scalar(rstd[par][0:rows, 0:t], mv[par][0:rows, 0:t, 1], EPS, None, ALU.add)\
                    .then_inc(s_var, 1)
                if not isinstance(c, int) or c:
                    finish(c - 1, turn if par else turn - 1, 1 - par, P, TPP)
            chunks(dve, body)
            finish(NCH, NCH // 2, 0, REST, 1)

        @block.scalar
        def _(act):
            def body(c, turn, par, rows, t):
                act.wait_ge(s_o, c + 1)
                dst = out_v[c] if rows == P else out[N - REST:N, :].unsqueeze(1)
                act.dma_start(dst, o[par][0:rows, 0:t, :]).then_inc(s_st[par], 16)
            chunks(act, body)
            act.wait_ge(s_st[0], (NCH // 2 + 1) * 16)
            act.wait_ge(s_st[1], NCH // 2 * 16)


def build(nc, d, out):
    d = dict(d)
    d["x1"] = nc.dram_tensor("x1_tokens", [N, C], F32).ap()
    d["lists"] = nc.dram_tensor("expert_lists", [NSLOT, ROW], F32).ap()
    d["y"] = nc.dram_tensor("expert_results", [K2 * N, C], F32).ap()
    attention_block(nc, d)
    expert_block(nc, d)
    last_block(nc, d, out)


def kernel(x, L0_tok_W, L0_tok_b, L0_tok_class_token, L0_tok_pos_emb, L0_attn_w_attn,
           L0_attn_b_attn, L0_attn_w_proj, L0_attn_b_proj, L0_ffn_Wg, L0_ffn_W1, L0_ffn_W2):
    import ml_dtypes
    import numpy as np
    import concourse.bacc as bacc
    from concourse.bass_utils import run_bass_kernel_spmd

    f32, bf16 = np.float32, ml_dtypes.bfloat16
    ins = {}

    px = np.asarray(x).reshape(B, 14, 16, 14, 16, 3).transpose(2, 4, 5, 0, 1, 3)
    px = px.reshape(KT, P, NPAIR, 2, T - 1)
    xt = np.zeros((NPAIR, P, KT, 2, TI), f32)
    xt[..., 1:T] = px.transpose(2, 1, 0, 3, 4)
    ins["xt"] = xt.reshape(NPAIR, P, KT, TP)
    ins["wtok"] = np.asarray(L0_tok_W).reshape(KT, P, C).transpose(1, 0, 2)

    def feature_tiles(w):
        return np.stack([w[:P], np.concatenate([w[P:], w[P:]])], axis=1)

    heads = np.arange(C).reshape(3, 64)
    order = np.concatenate([np.concatenate([g, C + g]) for g in heads] + [2 * C + np.arange(C)])
    wa, ba = np.asarray(L0_attn_w_attn)[:, order], np.asarray(L0_attn_b_attn)[order]
    wp, bp = np.asarray(L0_attn_w_proj), np.asarray(L0_attn_b_proj)
    ins["raw"] = np.concatenate([feature_tiles(wa).reshape(P, -1), feature_tiles(wp).reshape(P, -1)], axis=1)
    ins["bqk"] = ba[:2 * C].reshape(3, P).T
    ins["bv"] = np.broadcast_to(ba[2 * C:], (P, C))
    ins["bp"] = np.broadcast_to(bp, (P, C))

    def token_tiles(t):
        full = np.zeros((2 * P, C), f32)
        full[:T] = t
        return full.reshape(2, P, C).transpose(1, 0, 2)

    ins["pos"] = token_tiles(np.asarray(L0_tok_pos_emb))
    ins["bias"] = token_tiles(np.concatenate([np.asarray(L0_tok_class_token)[None],
                                              np.broadcast_to(np.asarray(L0_tok_b), (T - 1, C))]))
    wg = np.asarray(L0_ffn_Wg)
    ins["wg0"], ins["wg1"] = wg[:P], wg[P:]

    w1, w2 = np.asarray(L0_ffn_W1), np.asarray(L0_ffn_W2)
    wexp = np.stack([np.concatenate([
        feature_tiles(w1[e % E]).reshape(P, -1),
        w2[e % E].reshape(HM, P, C).transpose(1, 0, 2).reshape(P, -1)], axis=1) for e in range(E + 2)])
    ins["wexp"] = wexp

    sel = np.zeros((P, 2, 2, 2, P), bf16)
    for jj in range(2):
        for hh in range(2):
            for r in range(4):
                for e in range(HD):
                    src, dst = HD * (2 * jj + hh) + e, 64 * hh + HD * r + e
                    sel[src, 0, jj, r % 2, dst] = 1
                    sel[64 + src, 1, jj, r // 2, dst] = 1
    ins["sel"] = sel.reshape(P, 8 * P)
    row2 = np.zeros((2, 2, P), bf16)
    row2[0, 0], row2[1, 1] = 1, 1
    ins["row2"] = row2.reshape(2, 2 * P)
    n = np.arange(P)
    ins["ident"] = np.eye(P, dtype=f32)
    ins["masks"] = np.stack([np.eye(P), np.where(n[None] > n[:, None], -1e30, 0.0), np.ones((P, P)),
                             n[:, None] < n[None]], axis=1).astype(bf16)
    ins["iota8"] = np.broadcast_to(np.arange(E, dtype=f32), (P, E))
    ins["kbase"] = np.broadcast_to(np.arange(K2, dtype=f32) * SEG, (P, 4, K2))
    ins["valid"] = np.stack([n < r for r in REAL], axis=1).astype(f32)
    ins["tid"] = np.stack([im * T + hf * P + n for im, hf, _, _ in TILES], axis=1).astype(f32)

    nc = bacc.Bacc("TRN2", target_bir_lowering=False, num_devices=1)
    arrays, d = {}, {}
    for name, value in ins.items():
        arrays[f"in_{name}"] = np.ascontiguousarray(value)
        d[name] = nc.dram_tensor(f"in_{name}", value.shape, mybir.dt.from_np(value.dtype),
                                 kind="ExternalInput").ap()
    out = nc.dram_tensor("out", [N, C], F32, kind="ExternalOutput").ap()
    build(nc, d, out)
    r = run_bass_kernel_spmd(nc, [arrays], core_ids=[0])
    return r.results[0]["out"].reshape(B, T, C)
```

```python
from contextlib import ExitStack

import concourse.bass as bass
from concourse import mybir

F32 = mybir.dt.float32
F32R = mybir.dt.float32r
F16 = mybir.dt.float16
BF16 = mybir.dt.bfloat16
I32 = mybir.dt.int32
U32 = mybir.dt.uint32
ALU = mybir.AluOpType
ACT = mybir.ActivationFunctionType
AX = mybir.AxisListType

P = 128
B, T, C = 64, 197, 192
N = B * T
NH, HD = 12, 16
KT = 768 // P
C2 = C - P
NPAIR = B // 2
TI = T + 1
TP = 2 * TI
T1 = TI - P
STEPS = NH
NSTEP = NPAIR * STEPS
E, K2 = 8, 2
HID = 512
CAP = int(1.2 * N / E)
TILE3 = 3 * P
SEG = -(-CAP // TILE3) * TILE3
NSLOT = E * K2 * SEG
ROW = C + 2
FAR = 1.0e6
EPS = 1e-5
SCALE = HD ** -0.5
VW = HD + 1
HM = HID // P
WCOLS = 2 * 2 * HID + HM * C
NWORDS = 256
TRIES = 3

TILES = [(im, hf, im * TI + hf * P, T1 if hf else P) for im in range(2) for hf in range(2)]
REAL = [T - P if hf else P for _, hf, _, _ in TILES]

PIECES = [
    (1, 1, "QK0", 0), (2, 1, "QK1", 1), (2, 1, "QK2", 0), (3, 1, "SL0", 1), (3, 1, "SL1", 0),
    (4, 3, "TY0", 1), (4, 3, "TY1", 0), (4, 1, "SL2", 1), (4, 1, "SL3", 0), (5, 3, "PR0", 1),
    (5, 1, "SL4", 0), (6, 3, "PR1", 1), (6, 1, "SL5", 0), (7, 1, "V0", 1), (7, 1, "SL6", 0),
    (8, 3, "TR0", 1), (8, 3, "TR1", 0), (8, 1, "SL7", 1), (9, 3, "LG", 0), (9, 1, "SL8", 1),
    (9, 1, "V1", 0), (10, 1, "SL9", 1), (10, 1, "SL10", 0), (10, 1, "V2", 1), (11, 3, "RT", 0),
    (11, 1, "SL11", 1), (11, 1, "V3", 0),
]
EMBED = {5: (0, 0), 6: (0, 2), 7: (0, 4), 9: (1, 0), 10: (1, 2), 11: (1, 4)}


def stages_of(i):
    return tuple(k for k in (1, 2, 3, 4) if 0 <= i - (k - 1) < NPAIR)


def uses(bank, stages, before=None):
    names = [n for _, _, n, _ in PIECES]
    upto = names.index(before) if before else len(names)
    return sum(1 for _, st, _, b in PIECES[:upto] if b == bank and st in stages)


def uses_before(i, bank):
    if isinstance(i, int):
        return sum(uses(bank, stages_of(n)) for n in range(i))
    return i * uses(bank, (1, 3)) + (uses_before(2, bank) - 2 * uses(bank, (1, 3)))


def run_bodies(eng, body):
    for i in range(4):
        body(i, i // 2, i % 2, stages_of(i))
    with eng.Fori(2, NPAIR // 2) as it:
        for par in range(2):
            body(it * 2 + par, it, par, (1, 2, 3, 4))
    for i in range(NPAIR, NPAIR + 3):
        body(i, i // 2, i % 2, stages_of(i))


def wait(eng, sem, value):
    if not (isinstance(value, int) and value <= 0):
        eng.wait_ge(sem, value)


class Words:

    def __init__(self, eng, words):
        self.eng, self.words, self.n = eng, words, 0

    def wait(self, *waits):
        for sem, value in waits:
            wait(self.eng, sem, value)
        self.n += 1
        w = self.words
        self.eng.tensor_tensor(w[:, self.n:self.n + 1], w[:, 0:1], w[:, 0:1], ALU.add)


def is_step(n):
    return not isinstance(n, int) or 0 <= n < NSTEP


class Banks:

    def __init__(self, i, stages, full, drained):
        self.i, self.stages, self.full, self.drained = i, stages, full, drained
        self.bank = {name: b for _, _, name, b in PIECES}

    def pieces(self, step):
        return [name for s, st, name, _ in PIECES if s == step and st in self.stages]

    def count(self, name):
        b = self.bank[name]
        return uses_before(self.i, b) + uses(b, self.stages, name)

    def wait_free(self, eng, name):
        wait(eng, self.drained[self.bank[name]], self.count(name))

    def wait_full(self, eng, name):
        wait(eng, self.full[self.bank[name]], self.count(name) + 1)

    def is_drained(self, name):
        return self.drained[self.bank[name]], self.count(name) + 1

    def wait_drained(self, eng, name):
        wait(eng, *self.is_drained(name))


class Chain:

    def __init__(self, eng, sem, base):
        self.eng, self.sem, self.base, self.n = eng, sem, base, 0

    def mark(self, ins):
        self.n += 1
        return ins.then_inc(self.sem, 1)

    def sync(self):
        wait(self.eng, *self.last())

    def last(self):
        return self.sem, self.base + self.n


def repeat(ap, n):
    s = list(ap.shape)
    return ap.unsqueeze(1).broadcast_to([s[0], n] + s[1:])


def attention_block(nc, d):
    with ExitStack() as ctx:
        def sb(name, shape, dt):
            return ctx.enter_context(nc.sbuf_tensor(name, shape, dt))

        def sem(name):
            return ctx.enter_context(nc.semaphore(name))

        wtok_hi, wtok_lo = (sb(n, [P, KT, 2 * P], F32R) for n in ("wtok_hi", "wtok_lo"))
        wa_hi, wa_lo = sb("wa_hi", [P, 2, 4 * C], F32R), sb("wa_lo", [P, 2, 4 * C], F32R)
        wp_hi, wp_lo = sb("wp_hi", [P, 2, C], F32R), sb("wp_lo", [P, 2, C], F32R)
        wg0, wg1 = sb("wg0", [P, E], F32), sb("wg1", [C2, E], F32)
        bqk = sb("bqk", [P, 3], F32)
        bvp = sb("bvp", [P, 2 * C], F32)
        postab, biastab = sb("postab", [P, 2, TI], F32), sb("biastab", [P, 2, TI], F32)
        addend = sb("addend", [P, 2, TI], F32)
        selb = sb("selb", [P, 8 * P], BF16)
        sel = sb("sel", [P, 8, P], F32R)
        ones = sb("ones", [P, P], F32R)
        ident = sb("ident", [P, P], F32)
        masks = sb("masks", [P, 4, P], BF16)
        identb, maskb, onesb, lowb = (masks[:, n, :] for n in range(4))
        iota8, kbase = sb("iota8", [P, E], F32), sb("kbase", [P, 4, K2], F32)
        valid, tid = sb("valid", [P, 4], F32), sb("tid", [P, 4], F32)
        half = sb("half", [P, 4], F32)
        blank = sb("blank", [P, K2, TRIES, ROW], F32)
        zeros = sb("zeros", [P, C], F32)
        word_v, word_p = sb("word_v", [1, NWORDS], F32), sb("word_p", [1, NWORDS], F32)
        x = [sb(f"x{n}", [P, KT, TP], F32) for n in range(2)]
        x_hi, x_lo = (sb(n, [P, KT, TP], F32R) for n in ("x_hi", "x_lo"))
        ht = [sb(f"ht{n}", [P, TP], F32) for n in range(2)]
        h0_hi, h0_lo, h1 = (sb(n, [P, TP], F32R) for n in ("h0_hi", "h0_lo", "h1"))
        qk_hi = [sb(f"qk_hi{n}", [P, TP], F32R) for n in range(3)]
        qk_lo = [sb(f"qk_lo{n}", [P, TP], F32R) for n in range(3)]
        qs = [sb(f"qs{n}", [P, NH // 2, TP], F32R) for n in range(2)]
        ks = [sb(f"ks{n}", [P, NH // 2, TP], F32R) for n in range(2)]
        vh = [sb(f"vh{n}", [P, 4, 2 * C], F32) for n in range(2)]
        raw = x[1][:].rearrange("p a b -> p (a b)")[:, 0:2 * 5 * C]
        wtok = vh[1][:].rearrange("p a b -> p (a b)").rearrange("p (a b) -> p a b", a=KT)
        assert 4 * 2 * C == KT * 2 * P
        vrest, y_twice = sb("vrest", [P, 4, C], F32), sb("y_twice", [P, 4, P], F32)
        vs = [sb(f"vs{n}", [P, 4, NH, 3, VW], BF16) for n in range(2)]
        rmax = [sb(f"rmax{n}", [P, 2, 2], F32) for n in range(2)]
        shift = [sb(f"shift{n}", [P, 2, TI], F32R) for n in range(2)]
        p32 = [sb(f"p32_{n}", [P, 2, TI + T1], F32) for n in range(2)]
        p_hi = [sb(f"p_hi{n}", [P, 2, TI + T1], F16) for n in range(2)]
        p_lo = [sb(f"p_lo{n}", [P, 2, TI + T1], F16) for n in range(2)]
        ys = sb("ys", [P, 2, NH, VW], F32)
        rden = sb("rden", [P, 2, NH], F32)
        y32 = [sb(f"y32_{n}", [P, 4, C], F32) for n in range(2)]
        y0_hi, y0_lo, y1 = (sb(n, [P, TP], F32R) for n in ("y0_hi", "y0_lo", "y1"))
        r = sb("r", [P, 4, C], F32)
        stats, mv = sb("stats", [P, 4, 6], F32), sb("mv", [P, 4, 2], F32)
        rstd = sb("rstd", [P, 4], F32)
        pay = [sb(f"pay{n}", [P, 4, C + 4], F32) for n in range(2)]
        xt0, xt1 = sb("xt0", [P, TP], F32), sb("xt1", [C2, TP], F32)
        logit, top = sb("logit", [P, 4, E], F32), sb("top", [P, 4, E], F32)
        topi = sb("topi", [P, 4, E], U32)
        idf, rank, over, sl = (sb(n, [P, 4, K2], F32) for n in ("idf", "rank", "over", "sl"))
        slot = [sb(f"slot{n}", [P, 4, K2], I32) for n in range(2)]
        oh = sb("oh", [P, 4, K2, E], F32)
        ohb, acc = sb("ohb", [P, 4, K2 * E], BF16), sb("acc", [P, 5, K2 * E], BF16)
        pos, po = sb("pos", [P, 4, K2 * E], F32), sb("po", [P, 4, K2 * E], F32)
        carry = sb("carry", [P, K2 * E], F32)
        dif, ex, den = (sb(n, [P, 4], F32) for n in ("dif", "ex", "den"))

        G = [ctx.enter_context(nc.psum_tensor(f"G{n}", [P, 512], F32)) for n in range(2)]
        PV = ctx.enter_context(nc.psum_tensor("PV", [P, 512], F32))
        EB = ctx.enter_context(nc.psum_tensor("EB", [P, 512], F32))
        S = ctx.enter_context(nc.psum_tensor("S", [P, 2, 512], F32))
        ST = ctx.enter_context(nc.psum_tensor("ST", [P, 2, 512], F32))

        s_w, s_const = sem("weights_loaded"), sem("constants_ready")
        s_whi, s_set = sem("weights_hi"), sem("buffers_set")
        s_blank, s_clear = sem("blank_ready"), sem("dram_cleared")
        full = [sem("general0_full"), sem("general1_full")]
        drained = [sem("general0_drained"), sem("general1_drained")]
        s_x = [sem("x0_loaded"), sem("x1_loaded")]
        s_hi1, s_hi3 = sem("hi_part1"), sem("hi_part3")
        s_ytwice = sem("y_columns_twice")
        s_ef, s_ed = sem("embedded"), sem("embedding_drained")
        s_xhi, s_xlo, s_hlo = sem("x_hi_part"), sem("x_split"), sem("h_split")
        s_vstep, s_vsplit = sem("v_rest"), sem("v_split")
        s_vhi = sem("v_rounded")
        s_d2, s_d3 = sem("vector_step2"), sem("vector_step3")
        s_s, s_m = sem("scores_full"), sem("max_ready")
        s_sh, s_shz = sem("shift_ready"), sem("shift_zeros")
        s_st, s_exp = sem("turned_scores_full"), sem("exp_ready")
        s_mask, s_phi, s_plo = sem("p_masked"), sem("p_hi_ready"), sem("p_lo_ready")
        s_pv, s_pvt, s_y = sem("pv_full"), sem("pv_taken"), sem("y_ready")
        s_var, s_rstd = sem("variance_ready"), sem("rstd_ready")
        s_dif, s_ex = sem("gate_difference"), sem("gate_exp")
        s_wsplit, s_vhset = sem("weights_split"), sem("vh1_set")
        s_x1, s_slot = sem("x1_ready"), sem("slots_ready")
        s_st1 = [sem("x1_stored0"), sem("x1_stored1")]
        s_sc = [sem("rows_scattered0"), sem("rows_scattered1")]

        loads = [(wg0, "wg0"), (wg1, "wg1"), (bqk, "bqk"),
                 (bvp, "bvp"), (postab, "pos"), (biastab, "bias"), (selb, "sel"),
                 (ident, "ident"), (masks, "masks"), (iota8, "iota8"),
                 (kbase, "kbase"), (valid, "valid"), (tid, "tid")]
        SETS = 17
        NCLEAR = E * K2 + 1
        READY = 5
        XSTEPS = range(KT)

        def body_at(i):
            return Banks(i, stages_of(i) if isinstance(i, int) else (1, 2, 3, 4), full, drained)

        def v_parts(par):
            part = [vs[par][:, :, :, c, 0:HD] for c in range(3)]
            return (part, vh[par][:, :, 0:C].rearrange("p t (h e) -> p t h e", e=HD),
                    vrest[:].rearrange("p t (h e) -> p t h e", e=HD))

        block = ctx.enter_context(nc.Block())

        @block.sync
        def _(sp):
            sp.dma_start(wtok, d["wtok"]).then_inc(s_w, 16)
            sp.dma_start(raw, d["raw"]).then_inc(s_w, 16)
            for dst, name in loads:
                sp.dma_start(dst[:], d[name]).then_inc(s_w, 16)
            sp.dma_start(x[0][:], d["xt"][0]).then_inc(s_x[0], 16)
            sp.wait_ge(s_wsplit, 1)
            sp.dma_start(x[1][:], d["xt"][1]).then_inc(s_x[1], 16)

            def body(i, turn, par, stages):
                if 1 in stages:
                    sp.wait_ge(s_xlo, (i + 1) * KT)
                    sp.dma_start(x[par][:], d["xt"][i + 2]).then_inc(s_x[par], 16)
                if 3 in stages:
                    p = i - 2
                    sp.wait_ge(s_x1, p + 1)
                    for n, (im, hf, _, _) in enumerate(TILES):
                        sp.dma_start(d["x1"][bass.ds(p * (2 * T) + (im * T + hf * P), REAL[n]), :],
                                     pay[par][0:REAL[n], n, 2:2 + C]).then_inc(s_st1[par], 16)
            run_bodies(sp, body)
            for par in range(2):
                sp.wait_ge(s_st1[par], NPAIR // 2 * 4 * 16)
                sp.wait_ge(s_x[par], (NPAIR // 2 + 1) * 16)

        @block.gpsimd
        def _(pool):
            for t, value in ((vh[0], 0.0), (logit, 0.0), (r, 0.0), (ys, 1.0), (half, -0.5),
                             (acc, 0.0), (carry, 0.0), (zeros, 0.0), (p32[0], 0.0), (p32[1], 0.0),
                             (pay[0], 0.0), (pay[1], 0.0), (vs[0], 0.0), (vs[1], 0.0), (blank, 0.0),
                             (word_v, 0.0), (word_p, 0.0)):
                pool.memset(t[:], value).then_inc(s_set, 1)
            pool.wait_ge(s_set, SETS)
            words = Words(pool, word_p)
            for n in range(2):
                pool.memset(vs[n][:, :, :, 0, HD:VW], 1.0).then_inc(s_const, 1)
                c = ROW - 1 if n == 0 else 1
                pool.memset(blank[:, n, :, c:c + 1], FAR).then_inc(s_blank, 1)

            def x_rest(p, q, k):
                pool.wait_ge(s_xhi, p * KT + (k + 1))
                pool.tensor_tensor(x_lo[:, k], x[q][:, k], x_hi[:, k].bitcast(F32), ALU.subtract)\
                    .then_inc(s_xlo, 1)

            pool.wait_ge(s_wsplit, 1)
            pool.memset(vh[1][:], 0.0).then_inc(s_vhset, 1)
            for k in range(KT):
                x_rest(0, 0, k)

            def body(i, turn, par, stages):
                for s in range(STEPS):
                    n = (i - 1) * STEPS + s - 2
                    if s == 7 and 3 in stages:
                        pool.wait_ge(s_var, i - 1)
                        pool.tensor_tensor(rstd[:], rstd[:], half[:], ALU.pow).then_inc(s_rstd, 1)
                    if (2 in stages or s < 2) and is_step(n):
                        b = s % 2
                        words.wait((s_exp, n + 1))
                        pool.affine_select(out=p32[b][:, :, 0:P], in_=p32[b][:, :, 0:P],
                                           compare_op=ALU.is_ge, fill=0.0, base=0,
                                           pattern=[[0, 2], [1, P]], channel_multiplier=-1)\
                            .then_inc(s_mask, 1)
                        pool.affine_select(out=p32[b][0:T1, :, TI:TI + T1],
                                           in_=p32[b][0:T1, :, TI:TI + T1],
                                           compare_op=ALU.is_ge, fill=0.0, base=0,
                                           pattern=[[0, 2], [1, T1]], channel_multiplier=-1)\
                            .then_inc(s_mask, 1)
                    if s < 8 and 4 in stages:
                        p, o = i - 3, 1 - par
                        t, k = s // 2, s % 2
                        if s == 0:
                            words.wait((s_clear, 16 * NCLEAR), (s_slot, p + 1))
                        first = 2 if k == 0 else 0
                        pool.indirect_dma_start(
                            d["lists"][:, :],
                            bass.IndirectOffsetOnAxis(ap=slot[o][0:REAL[t], t, k:k + 1], axis=0),
                            pay[o][0:REAL[t], t, first:first + ROW], None,
                            bounds_check=NSLOT - 1, oob_is_err=False).then_inc(s_sc[o], 16)
                    if s in XSTEPS and 1 in stages:
                        x_rest(i + 1, 1 - par, s - XSTEPS[0])
                if 1 in stages:
                    part, v3, r3 = v_parts(par)
                    pool.wait_ge(s_vhi, i * 2 + 1)
                    pool.tensor_tensor(r3, v3, part[0], ALU.subtract).then_inc(s_vstep, 1)
                    pool.wait_ge(s_vhi, i * 2 + 2)
                    pool.tensor_tensor(part[2], r3, part[1], ALU.subtract).then_inc(s_vsplit, 1)
            run_bodies(pool, body)
            for par in range(2):
                pool.wait_ge(s_sc[par], NPAIR // 2 * 8 * 16)

        @block.scalar
        def _(act):
            act.wait_ge(s_blank, 2)
            act.wait_ge(s_set, SETS)
            for e in range(E):
                for k in range(K2):
                    at = (e * K2 + k) * SEG
                    dst = d["lists"][at:at + SEG, :].rearrange("(p a t) c -> p a (t c)", p=P, t=TRIES)
                    src = blank[:, k].rearrange("p t c -> p (t c)")
                    act.dma_start(dst, repeat(src, SEG // P // TRIES)).then_inc(s_clear, 16)
            yd = d["y"].rearrange("(p t) c -> p (t c)", p=P)
            act.dma_start(yd.rearrange("p (a c) -> p a c", c=C), repeat(zeros[:], K2 * N // P))\
                .then_inc(s_clear, 16)
            act.wait_ge(s_w, 16 * (len(loads) + 2))
            act.activation(sel[:].rearrange("p a b -> p (a b)"), selb[:], ACT.Copy).then_inc(s_const, 1)
            act.activation(ones[:], onesb, ACT.Copy).then_inc(s_const, 1)
            for q in range(2):
                act.activation(shift[q][:, :, P:TI], repeat(zeros[:, 0:T1], 2), ACT.Copy)\
                    .then_inc(s_shz, 1)
            act.wait_ge(s_shz, 2)
            a = 2 * 4 * C
            act.activation(wa_hi[:].rearrange("p a b -> p (a b)"), raw[:, 0:a], ACT.Copy)\
                .then_inc(s_whi, 1)
            act.activation(wp_hi[:].rearrange("p a b -> p (a b)"), raw[:, a:], ACT.Copy)\
                .then_inc(s_whi, 1)
            act.activation(wtok_hi[:], wtok, ACT.Copy).then_inc(s_whi, 1)

            def x_round(q, k):
                act.activation(x_hi[:, k], x[q][:, k], ACT.Copy).then_inc(s_xhi, 1)

            act.wait_ge(s_x[0], 16)
            for k in range(KT):
                x_round(0, k)

            def twice(dst, src):
                return act.activation(dst[:].rearrange("p t (a b) -> p t a b", a=2),
                                      src[:, :, P:C].unsqueeze(2).broadcast_to([P, 4, 2, C2]), ACT.Copy)

            def hi_pair(g, name, dst, sem_):
                g.wait_full(act, name)
                act.activation(dst, G[g.bank[name]][:, 0:TP], ACT.Copy).then_inc(sem_, 1)

            def body(i, turn, par, stages):
                g = body_at(i)
                for s in range(STEPS):
                    n = (i - 1) * STEPS + s
                    if (2 in stages or s < 1) and is_step(n - 1):
                        act.wait_ge(s_m, n)
                        wait(act, s_st, n - 2)
                        q = (s - 1) % 2
                        for hh in range(2):
                            act.activation(shift[q][:, hh, 0:P], ident[:], ACT.Copy,
                                           scale=rmax[q][:, 0, hh:hh + 1])
                            ins = act.activation(shift[q][0:T1, hh, P:TI], ident[0:T1, 0:T1], ACT.Copy,
                                                 scale=rmax[q][0:T1, 1, hh:hh + 1])
                        ins.then_inc(s_sh, 1)
                    if (2 in stages or s < 2) and is_step(n - 2):
                        b = s % 2
                        act.wait_ge(s_st, n - 1)
                        wait(act, s_plo, n - 3)
                        act.activation(p32[b][:, :, 0:TI], ST[:, :, 0:TI], ACT.Exp, scale=SCALE)
                        act.activation(p32[b][0:T1, :, TI:TI + T1], ST[0:T1, :, TI:TI + T1],
                                       ACT.Exp, scale=SCALE).then_inc(s_exp, 1)
                    if s == 0 and 1 in stages:
                        for k in range(2):
                            act.wait_ge(s_ed, i * 2 + (k + 1))
                            act.activation((h0_hi, h1)[k][:], ht[k][:], ACT.Copy).then_inc(s_hi1, 1)
                    if s in XSTEPS and 1 in stages:
                        k = s - XSTEPS[0]
                        if k == 0:
                            act.wait_ge(s_ef, (i + 1) * 2)
                            act.wait_ge(s_x[1 - par], (turn + 1 + par) * 16)
                        x_round(1 - par, k)
                    for name in g.pieces(s):
                        src = G[g.bank[name]]
                        if name == "TY0":
                            hi_pair(g, name, y0_hi[:], s_hi3)
                        elif name == "TY1":
                            hi_pair(g, name, y1[:], s_hi3)
                        elif name[:2] == "QK":
                            t = int(name[2:])
                            g.wait_full(act, name)
                            act.activation(qk_hi[t][:], src[:, 0:TP], ACT.Identity,
                                           bias=bqk[:, t:t + 1]).then_inc(s_hi1, 1)
                        elif name[:2] == "SL" and int(name[2:]) % 2 == 0:
                            g.wait_full(act, name)
                            q = int(name[2:])
                            dst = qs if q % 4 < 2 else ks
                            act.activation(dst[par][:, 2 * (q // 4) + q % 2, :], src[:, 0:TP], ACT.Copy)\
                                .then_inc(drained[g.bank[name]], 1)
                        elif name == "TR0":
                            g.wait_full(act, name)
                            act.activation(xt0[:], src[:, 0:TP], ACT.Copy)\
                                .then_inc(drained[g.bank[name]], 1)
                        elif name == "TR1":
                            g.wait_full(act, name)
                            act.activation(xt1[:], src[0:C2, 0:TP], ACT.Copy)\
                                .then_inc(drained[g.bank[name]], 1)
                        elif name == "RT":
                            act.wait_ge(s_dif, i - 1)
                            act.activation(ex[:], dif[:], ACT.Exp).then_inc(s_ex, 1)
                    if s == 3 and 3 in stages:
                        act.wait_ge(s_y, (i - 1) * 2)
                        twice(y_twice, y32[par]).then_inc(s_ytwice, 1)
                    if (2 in stages or s < 2) and is_step(n - 2):
                        act.wait_ge(s_mask, n * 2 - 2)
                        wait(act, s_pv, n - 3)
                        act.activation(p_hi[s % 2][:], p32[s % 2][:], ACT.Copy).then_inc(s_phi, 1)
                if 1 in stages:
                    part, v3, r3 = v_parts(par)
                    g.wait_drained(act, "V2")
                    g.wait_drained(act, "V3")
                    act.activation(part[0], v3, ACT.Copy).then_inc(s_vhi, 1)
                    act.wait_ge(s_vstep, i + 1)
                    act.activation(part[1], r3, ACT.Copy).then_inc(s_vhi, 1)
            run_bodies(act, body)
            act.wait_ge(s_clear, 16 * NCLEAR)

        @block.tensor
        def _(pe):
            pe.wait_ge(s_w, 16 * (len(loads) + 2))
            pe.wait_ge(s_const, READY)
            pe.wait_ge(s_wsplit, 1)

            def turned(g, name, src, first, width=P):
                g.wait_free(pe, name)
                b = g.bank[name]
                for t, (_, _, col, rows) in enumerate(TILES):
                    mm = pe.transpose(G[b][0:width, col:col + rows],
                                      src[0:rows, t, first:first + width], ident[0:rows, 0:rows])
                mm.then_inc(full[b], 1)

            def five(out, lhs, rhs):
                for n in range(5):
                    mm = pe.matmul(out, lhs[n], rhs[n], start=(n == 0), stop=(n == 4))
                return mm

            def embed(p, ft, k0):
                if ft == 0:
                    pe.wait_ge(s_xlo, p * KT + (k0 + 2))
                if k0 == 0:
                    wait(pe, s_ed, p * 2 + ft)
                w = slice(ft * P, (ft + 1) * P)
                for k in (k0, k0 + 1):
                    for c, (wt, xp) in enumerate(((wtok_hi, x_hi), (wtok_lo, x_hi), (wtok_hi, x_lo))):
                        mm = pe.matmul(EB[:, 0:TP], wt[:, k, w], xp[:, k],
                                       start=(k == 0 and c == 0), stop=(k == KT - 1 and c == 2))
                if k0 == KT - 2:
                    mm.then_inc(s_ef, 1)

            for ft in range(2):
                for k0 in range(0, KT, 2):
                    embed(0, ft, k0)

            def body(i, turn, par, stages):
                g = body_at(i)
                pb = 1 - par
                for s in range(STEPS):
                    n = (i - 1) * STEPS + s
                    im, j = s // 6, s % 6
                    c0 = im * TI
                    if 2 in stages:
                        if s == 0:
                            body_at(i - 1).wait_drained(pe, "SL10")
                            body_at(i - 1).wait_drained(pe, "SL11")
                        wait(pe, s_m, n)
                        for hh in range(2):
                            hp = slice(64 * hh, 64 * hh + 64)
                            pe.matmul(S[:, hh, 0:P], qs[pb][hp, j, c0:c0 + P], ks[pb][hp, j, c0:c0 + P],
                                      start=True, stop=False)
                            pe.matmul(S[:, hh, 0:P], identb, maskb, start=False, stop=True)
                            pe.matmul(S[0:T1, hh, P:P + TI], qs[pb][hp, j, c0 + P:c0 + TI],
                                      ks[pb][hp, j, c0:c0 + TI], start=True, stop=False)
                            mm = pe.matmul(S[0:T1, hh, 2 * P:2 * P + T1], identb[0:T1, 0:T1],
                                           maskb[0:T1, 0:T1], start=False, stop=True)
                        mm.then_inc(s_s, 1)
                    if (2 in stages or s < 2) and is_step(n - 2):
                        s2 = (s - 2) % STEPS
                        im2, j2 = s2 // 6, s2 % 6
                        cc, b2 = im2 * TI, (pb if s >= 2 else par)
                        sh = shift[s % 2]
                        pe.wait_ge(s_sh, n - 1)
                        wait(pe, s_exp, n - 2)
                        for hh in range(2):
                            hp = slice(64 * hh, 64 * hh + 64)
                            pe.matmul(ST[:, hh, 0:TI], ones[:], sh[:, hh, :], start=True, stop=False)
                            pe.matmul(ST[:, hh, 0:TI], ks[b2][hp, j2, cc:cc + P],
                                      qs[b2][hp, j2, cc:cc + TI], start=False, stop=True)
                            pe.matmul(ST[0:T1, hh, TI:TI + T1], ks[b2][hp, j2, cc + P:cc + TI],
                                      qs[b2][hp, j2, cc + P:cc + TI], start=True, stop=False)
                            mm = pe.matmul(ST[0:T1, hh, TI:TI + T1], ones[0:T1, 0:T1],
                                           sh[0:T1, hh, P:TI], start=False, stop=True)
                        mm.then_inc(s_st, 1)
                    for name in g.pieces(s):
                        b = g.bank[name]
                        if name[:2] == "TY":
                            if name == "TY0":
                                pe.wait_ge(s_y, (i - 1) * 2)
                                turned(g, name, y32[par], 0)
                            else:
                                pe.wait_ge(s_ytwice, i - 1)
                                turned(g, name, y_twice, 0)
                        elif name[:2] == "TR":
                            if name == "TR0":
                                pe.wait_ge(s_x1, i - 1)
                                turned(g, name, pay[par], 2)
                            else:
                                turned(g, name, pay[par], 2 + P, C2 + 2)
                        elif name[:2] == "QK":
                            t = int(name[2])
                            if t == 0:
                                pe.wait_ge(s_hlo, (i + 1) * 2)
                            g.wait_free(pe, name)
                            w = slice(t * P, (t + 1) * P)
                            five(G[b][:, 0:TP],
                                 [wa_hi[:, 0, w], wa_hi[:, 0, w], wa_lo[:, 0, w], wa_hi[:, 1, w],
                                  wa_lo[:, 1, w]],
                                 [h0_hi[:], h0_lo[:], h0_hi[:], h1[:], h1[:]]).then_inc(full[b], 1)
                        elif name[:2] == "SL":
                            q = int(name[2:])
                            t, which, jj = q // 4, (q % 4) // 2, q % 2
                            g.wait_drained(pe, f"QK{t}")
                            g.wait_free(pe, name)
                            for part in range(2):
                                mm = pe.matmul(G[b][:, 0:TP], sel[:, 4 * which + 2 * jj + part, :],
                                               (qk_lo if part else qk_hi)[t][:],
                                               start=(part == 0), stop=(part == 1))
                            mm.then_inc(full[b], 1)
                        elif name[0] == "V":
                            g.wait_free(pe, name)
                            _, _, col, rows = TILES[int(name[1])]
                            c = slice(col, col + rows)
                            w, v = slice(2 * C, 4 * C), slice(2 * C, 3 * C)
                            out, outv = G[b][0:rows, 0:2 * C], G[b][0:rows, 0:C]
                            pe.matmul(out, h0_hi[:, c], wa_hi[:, 0, w], start=True, stop=False)
                            pe.matmul(outv, h0_hi[:, c], wa_lo[:, 0, v], start=False, stop=False)
                            pe.matmul(out, h0_lo[:, c], wa_hi[:, 0, w], start=False, stop=False)
                            pe.matmul(outv, h1[:, c], wa_lo[:, 1, v], start=False, stop=False)
                            pe.matmul(out, h1[:, c], wa_hi[:, 1, w], start=False, stop=True)\
                                .then_inc(full[b], 1)
                        elif name[:2] == "PR":
                            if name == "PR0":
                                g.wait_drained(pe, "TY0")
                                g.wait_drained(pe, "TY1")
                            g.wait_free(pe, name)
                            for hf in range(2):
                                _, _, col, rows = TILES[2 * int(name[2]) + hf]
                                c = slice(col, col + rows)
                                mm = five(G[b][0:rows, hf * C:(hf + 1) * C],
                                          [y0_hi[:, c], y0_lo[:, c], y0_hi[:, c], y1[:, c], y1[:, c]],
                                          [wp_hi[:, 0], wp_hi[:, 0], wp_lo[:, 0], wp_hi[:, 1],
                                           wp_lo[:, 1]])
                            mm.then_inc(full[b], 1)
                        elif name == "LG":
                            g.wait_drained(pe, "TR0")
                            g.wait_drained(pe, "TR1")
                            g.wait_free(pe, name)
                            for t, (_, _, col, rows) in enumerate(TILES):
                                o = G[b][0:rows, t * E:(t + 1) * E]
                                pe.matmul(o, xt0[:, col:col + rows], wg0[:], start=True, stop=False)
                                mm = pe.matmul(o, xt1[:, col:col + rows], wg1[:], start=False, stop=True)
                            mm.then_inc(full[b], 1)
                        elif name == "RT":
                            pe.wait_ge(s_dif, i - 1)
                            g.wait_free(pe, name)
                            w = 4 * K2 * E
                            pe.matmul(G[b][:, 0:w], onesb, acc[:, 0:4].rearrange("p a b -> p (a b)"),
                                      start=True, stop=False)
                            pe.matmul(G[b][:, 0:w], lowb, ohb[:].rearrange("p a b -> p (a b)"),
                                      start=False, stop=True)
                            pe.matmul(G[b][:, w:w + K2 * E], onesb, acc[:, 4], start=True, stop=True)\
                                .then_inc(full[b], 1)
                    if 1 in stages and s in EMBED:
                        embed(i + 1, *EMBED[s])
                    if (2 in stages or s < 3) and is_step(n - 3):
                        s3 = (s - 3) % STEPS
                        im3, j3 = s3 // 6, s3 % 6
                        b3, q = (pb if s >= 3 else par), (s - 3) % 2
                        pe.wait_ge(s_plo, n - 2)
                        wait(pe, s_pvt, n - 3)
                        if s3 == 0:
                            pe.wait_ge(s_vsplit, i - (0 if s >= 3 else 1))
                        for hh in range(2):
                            hd = 2 * j3 + hh
                            v0 = vs[b3][:, 2 * im3, hd].rearrange("p a b -> p (a b)")
                            v1 = vs[b3][0:T1, 2 * im3 + 1, hd].rearrange("p a b -> p (a b)")
                            o0 = PV[:, hh * 3 * VW:(hh + 1) * 3 * VW]
                            o1 = PV[0:T1, P + hh * 3 * VW:P + (hh + 1) * 3 * VW]
                            pe.matmul(o0, p_hi[q][:, hh, 0:P], v0, start=True, stop=False)
                            pe.matmul(o0, p_lo[q][:, hh, 0:P], v0, start=False, stop=True)
                            pe.matmul(o1, p_hi[q][:, hh, P:TI], v0, start=True, stop=False)
                            pe.matmul(o1, p_lo[q][:, hh, P:TI], v0, start=False, stop=False)
                            pe.matmul(o1, p_hi[q][0:T1, hh, TI:TI + T1], v1, start=False, stop=False)
                            mm = pe.matmul(o1, p_lo[q][0:T1, hh, TI:TI + T1], v1, start=False, stop=True)
                        mm.then_inc(s_pv, 1)
            run_bodies(pe, body)

        @block.vector
        def _(dve):
            dve.wait_ge(s_w, 16 * (len(loads) + 2))
            dve.tensor_tensor(addend[:], postab[:], biastab[:], ALU.add).then_inc(s_const, 1)
            dve.wait_ge(s_whi, 3)
            dve.tensor_tensor(wtok_lo[:], wtok, wtok_hi[:].bitcast(F32), ALU.subtract)
            a = 2 * 4 * C
            dve.tensor_tensor(wa_lo[:].rearrange("p a b -> p (a b)"), raw[:, 0:a],
                              wa_hi[:].rearrange("p a b -> p (a b)").bitcast(F32), ALU.subtract)
            dve.tensor_tensor(wp_lo[:].rearrange("p a b -> p (a b)"), raw[:, a:],
                              wp_hi[:].rearrange("p a b -> p (a b)").bitcast(F32), ALU.subtract)\
                .then_inc(s_wsplit, 1)
            dve.wait_ge(s_vhset, 1)
            dve.wait_ge(s_set, SETS)
            dve.wait_ge(s_const, READY)
            words = Words(dve, word_v)
            D3 = 23

            def rest(src, hi, lo, rows):
                return dve.tensor_tensor(lo[rows], src[rows, 0:TP], hi[rows].bitcast(F32), ALU.subtract)

            def embedded(p, k):
                dve.wait_ge(s_ef, p * 2 + (k + 1))
                wait(dve, s_hlo, p * 2)
                dve.scalar_tensor_tensor(
                    out=ht[k][:].rearrange("p (a b) -> p a b", a=2),
                    in0=EB[:, 0:TP].rearrange("p (a b) -> p a b", a=2),
                    scalar=1.0 / 255.0, in1=repeat(addend[:, k], 2),
                    op0=ALU.mult, op1=ALU.add).then_inc(s_ed, 1)

            embedded(0, 0)
            embedded(0, 1)

            def body(i, turn, par, stages):
                g = body_at(i)
                every, upper = slice(0, P), slice(C2, P)
                p = i - 2
                ch = Chain(dve, s_d3, p * D3)
                pb = pay[par]
                for s in range(STEPS):
                    n = (i - 1) * STEPS + s
                    if 2 in stages:
                        dve.wait_ge(s_s, n + 1)
                        wait(dve, s_sh, n - 1)
                        q = s % 2
                        dve.tensor_reduce(rmax[q][:, 0, :], S[:, :, 0:P], AX.X, ALU.max, negate=True)
                        dve.tensor_reduce(rmax[q][0:T1, 1, :], S[0:T1, :, P:P + TI], AX.X, ALU.max,
                                          negate=True).then_inc(s_m, 1)
                    for name in g.pieces(s):
                        b = g.bank[name]
                        src = G[b]
                        if name[:2] == "TY":
                            k = int(name[2])
                            dve.wait_ge(s_hi3, p * 2 + (k + 1))
                            hi, lo = (y0_hi, y0_lo) if k == 0 else (y1, y1)
                            rest(src, hi, lo, every if k == 0 else upper).then_inc(drained[b], 1)
                        elif name[:2] == "QK":
                            t = int(name[2])
                            dve.wait_ge(s_hi1, i * 5 + (t + 3))
                            dve.scalar_tensor_tensor(
                                out=qk_lo[t][:], in0=src[:, 0:TP], scalar=bqk[:, t:t + 1],
                                in1=qk_hi[t][:].bitcast(F32), op0=ALU.add, op1=ALU.subtract)\
                                .then_inc(drained[b], 1)
                        elif name[:2] == "SL" and int(name[2:]) % 2 == 1:
                            g.wait_full(dve, name)
                            q = int(name[2:])
                            dst = qs if q % 4 < 2 else ks
                            dve.tensor_copy(dst[par][:, 2 * (q // 4) + q % 2, :], src[:, 0:TP])\
                                .then_inc(drained[b], 1)
                        elif name[0] == "V":
                            g.wait_full(dve, name)
                            wait(dve, s_vsplit, i - 1)
                            t = int(name[1])
                            rows = TILES[t][3]
                            dve.tensor_tensor(vh[par][0:rows, t, :], src[0:rows, 0:2 * C],
                                              bvp[0:rows, :], ALU.add).then_inc(drained[b], 1)
                        elif name[:2] == "PR":
                            g.wait_full(dve, name)
                            for hf in range(2):
                                t = 2 * int(name[2]) + hf
                                rows = TILES[t][3]
                                ins = dve.tensor_tensor(r[0:rows, t, :],
                                                        src[0:rows, hf * C:(hf + 1) * C],
                                                        vh[par][0:rows, t, C:2 * C], ALU.add)
                            ins.then_inc(drained[b], 1)
                            if name == "PR1":
                                g.wait_drained(dve, "PR0")
                                g.wait_drained(dve, "PR1")
                                for t in range(4):
                                    ins = dve.bn_stats(stats[:, t, :], r[:, t, :])
                                ch.mark(ins)
                                words.wait(ch.last())
                                for t in range(4):
                                    ins = dve.bn_aggr(mv[:, t, :], stats[:, t, :])
                                ch.mark(ins)
                                ch.sync()
                                dve.tensor_scalar(rstd[:], mv[:, :, 1], EPS, None, ALU.add)\
                                    .then_inc(s_var, 1)
                        elif name == "LG":
                            g.wait_full(dve, name)
                            lv = src[:, 0:4 * E].rearrange("p (a b e) -> p a b e", b=2, e=E)
                            dst = logit[:].rearrange("p (a b) e -> p a b e", b=2)
                            dve.tensor_copy(dst[:, :, 0], lv[:, :, 0])
                            dve.tensor_copy(dst[0:T1, :, 1], lv[0:T1, :, 1]).then_inc(drained[b], 1)
                            words.wait(g.is_drained("LG"))
                            for t in range(4):
                                ins = dve.max(top[:, t, :], logit[:, t, :])
                            ch.mark(ins)
                            words.wait(ch.last())
                            for t in range(4):
                                ins = dve.max_index(topi[:, t, :], top[:, t, :], logit[:, t, :])
                            ch.mark(ins)
                            ch.sync()
                            ch.mark(dve.tensor_copy(idf[:], topi[:, :, 0:K2]))
                            ch.sync()
                            ch.mark(dve.tensor_tensor(
                                oh[:], iota8[:].unsqueeze(1).unsqueeze(1).broadcast_to([P, 4, K2, E]),
                                idf[:].unsqueeze(3).broadcast_to([P, 4, K2, E]), ALU.is_equal))
                            ch.sync()
                            ch.mark(dve.tensor_tensor(
                                ohb[:], oh[:].rearrange("p a b c -> p a (b c)"),
                                valid[:].unsqueeze(2).broadcast_to([P, 4, K2 * E]), ALU.mult))
                            ch.sync()
                            for t in range(4):
                                ch.mark(dve.tensor_tensor(acc[:, t + 1], acc[:, t], ohb[:, t], ALU.add))
                                ch.sync()
                            dve.tensor_tensor(dif[:], top[:, :, 1], top[:, :, 0], ALU.subtract)\
                                .then_inc(s_dif, 1)
                        elif name == "RT":
                            g.wait_full(dve, name)
                            w = 4 * K2 * E
                            ch.mark(dve.tensor_tensor(
                                pos[:], src[:, 0:w].rearrange("p (a b) -> p a b", a=4),
                                repeat(carry[:], 4), ALU.add))
                            ch.sync()
                            dve.tensor_tensor(carry[:], src[:, w:w + K2 * E], carry[:], ALU.add)\
                                .then_inc(drained[b], 1)
                            ch.mark(dve.tensor_tensor(po[:], pos[:], ohb[:], ALU.mult))
                            ch.sync()
                            ch.mark(dve.tensor_reduce(
                                rank[:], po[:].rearrange("p a (b c) -> p a b c", b=K2), AX.X, ALU.add))
                            ch.mark(dve.scalar_tensor_tensor(
                                out=sl[:], in0=idf[:], scalar=float(K2 * SEG), in1=kbase[:],
                                op0=ALU.mult, op1=ALU.add))
                            ch.sync()
                            ch.mark(dve.tensor_scalar(over[:], rank[:], float(CAP), FAR,
                                                      ALU.is_ge, ALU.mult))
                            ch.mark(dve.tensor_tensor(sl[:], sl[:], rank[:], ALU.add))
                            ch.sync()
                            ch.mark(dve.tensor_tensor(slot[par][:], sl[:], over[:], ALU.add))
                            dve.wait_ge(s_ex, p + 1)
                            ch.mark(dve.tensor_scalar(den[:], ex[:], 1.0, None, ALU.add))
                            ch.sync()
                            ch.mark(dve.reciprocal(pb[:, :, C + 2], den[:]))
                            ch.mark(dve.tensor_copy(pb[:, :, C + 3], tid[:]))
                            ch.mark(dve.tensor_scalar(pb[:, :, 1], tid[:], float(N), None, ALU.add))
                            ch.sync()
                            ch.mark(dve.tensor_scalar(tid[:], tid[:], float(2 * T), None, ALU.add))
                            dve.tensor_tensor(pb[:, :, 0], ex[:], pb[:, :, C + 2], ALU.mult)\
                                .then_inc(s_slot, 1)
                            assert ch.n == D3, ch.n
                    if s == 0 and 1 in stages:
                        dve.wait_ge(s_hi1, i * 5 + 1)
                        dve.tensor_tensor(h0_lo[:], ht[0][:], h0_hi[:].bitcast(F32), ALU.subtract)\
                            .then_inc(s_hlo, 1)
                        dve.wait_ge(s_hi1, i * 5 + 2)
                        dve.tensor_tensor(h1[C2:P], ht[1][C2:P], h1[C2:P].bitcast(F32), ALU.subtract)\
                            .then_inc(s_hlo, 1)
                    if s == 8 and 1 in stages:
                        embedded(i + 1, 0)
                    if s == 7 and 3 in stages:
                        if not isinstance(i, int) or p >= 2:
                            dve.wait_ge(s_st1[par], (turn - 1) * 4 * 16)
                            dve.wait_ge(s_sc[par], (turn - 1) * 8 * 16)
                        dve.wait_ge(s_rstd, p + 1)
                        for t in range(4):
                            ins = dve.tensor_scalar(pb[:, t, 2:2 + C], r[:, t, :], mv[:, t, 0:1],
                                                    rstd[:, t:t + 1], ALU.subtract, ALU.mult)
                        ins.then_inc(s_x1, 1)
                    if (2 in stages or s < 2) and is_step(n - 2):
                        q = s % 2
                        dve.wait_ge(s_phi, n - 1)
                        dve.tensor_tensor(p_lo[q][:], p32[q][:], p_hi[q][:], ALU.subtract)\
                            .then_inc(s_plo, 1)
                    if (2 in stages or s < 3) and is_step(n - 3):
                        s3 = (s - 3) % STEPS
                        im3, j3 = s3 // 6, s3 % 6
                        dve.wait_ge(s_pv, n - 2)
                        if j3 == 0:
                            wait(dve, s_y, (i - 1 if s >= 3 else i - 2) * 2 + im3)
                        for hf, rows in ((0, P), (1, T1)):
                            v = PV[0:rows, hf * P:hf * P + 6 * VW]\
                                .rearrange("p (h c d) -> p h d c", h=2, c=3)
                            ins = dve.tensor_reduce(ys[0:rows, hf, 2 * j3:2 * j3 + 2, :], v, AX.X, ALU.add)
                        ins.then_inc(s_pvt, 1)
                        if j3 == 5:
                            y = y32[1 - par if s >= 3 else par]
                            dve.wait_ge(s_pvt, n - 2)
                            done = (i - 1 if s >= 3 else i - 2) * 2 + (im3 + 1)
                            dve.reciprocal(rden[:], ys[:, :, :, HD]).then_inc(s_d2, 1)
                            dve.wait_ge(s_d2, done)
                            for hf in range(2):
                                ins = dve.tensor_tensor(
                                    y[:, 2 * im3 + hf, :].rearrange("p (h e) -> p h e", e=HD),
                                    ys[:, hf, :, 0:HD],
                                    rden[:, hf].unsqueeze(2).broadcast_to([P, NH, HD]), ALU.mult)
                            ins.then_inc(s_y, 1)
                if 1 in stages:
                    embedded(i + 1, 1)
            run_bodies(dve, body)



def expert_block(nc, d):
    CPE = K2 * SEG // TILE3
    NC2 = 2 * CPE
    W1C = 2 * 2 * HID
    with ExitStack() as ctx:
        def sb(name, shape, dt):
            return ctx.enter_context(nc.sbuf_tensor(name, shape, dt))

        def sem(name):
            return ctx.enter_context(nc.semaphore(name))

        ident = sb("e_ident", [P, P], F32)
        word_p = sb("e_word", [1, NWORDS], F32)
        raw = [sb(f"e_raw{n}", [P, WCOLS], F32) for n in range(2)]
        w1_hi = [sb(f"w1_hi{n}", [P, 2, 2 * HID], F32R) for n in range(2)]
        w1_lo = [sb(f"w1_lo{n}", [P, 2, 2 * HID], F32R) for n in range(2)]
        w2 = [sb(f"w2_{n}", [P, HM, 2, C], F32R) for n in range(2)]
        rows = [sb(f"rows{n}", [P, 3, ROW], F32) for n in range(2)]
        twice = [sb(f"twice{n}", [P, 3, P], F32) for n in range(2)]
        wt = [sb(f"wt{n}", [P, 3], F32) for n in range(4)]
        target = [sb(f"target{n}", [P, 3], I32) for n in range(4)]
        x0_hi = [sb(f"ex0_hi{n}", [P, TILE3], F32R) for n in range(2)]
        x0_lo = [sb(f"ex0_lo{n}", [P, TILE3], F32R) for n in range(2)]
        x1 = [sb(f"ex1_{n}", [P, TILE3], F32R) for n in range(2)]
        gate = [sb(f"gate{n}", [P, TILE3], F32) for n in range(2)]
        a32 = [sb(f"a32_{n}", [P, TILE3], F32) for n in range(2)]
        a_hi = [sb(f"a_hi{n}", [P, HM, TILE3], F32R) for n in range(2)]
        a_lo = [sb(f"a_lo{n}", [P, HM, TILE3], F32R) for n in range(2)]
        ylo = [sb(f"ylo{n}", [P, C], F32) for n in range(2)]
        yout = [sb(f"yout{n}", [P, C], F32) for n in range(6)]

        XT = [ctx.enter_context(nc.psum_tensor(f"XT{n}", [P, 512], F32)) for n in range(2)]
        UP = [ctx.enter_context(nc.psum_tensor(f"UP{n}", [P, 512], F32)) for n in range(2)]
        GT = [ctx.enter_context(nc.psum_tensor(f"GT{n}", [P, 512], F32)) for n in range(2)]
        Y = [ctx.enter_context(nc.psum_tensor(f"Y{n}", [P, 512], F32)) for n in range(2)]

        s_id, s_word = sem("e_ident_loaded"), sem("e_word_set")
        s_raw = [sem("weights0_loaded"), sem("weights1_loaded")]
        s_whi, s_wlo = sem("e_weights_hi"), sem("e_weights_split")
        s_rows = [sem("rows0_loaded"), sem("rows1_loaded")]
        s_twice = sem("columns_twice")
        s_xt, s_xhi, s_split = sem("rows_turned"), sem("rows_hi"), sem("rows_split")
        s_ug, s_gate, s_a = sem("hidden_full"), sem("gate_ready"), sem("hidden_ready")
        s_ahi, s_alo = sem("hidden_hi"), sem("hidden_split")
        s_y, s_ylo, s_yout = sem("y_full"), sem("y_lo_scaled"), sem("y_out_ready")
        s_out = [sem(f"y_scattered{n}") for n in range(6)]

        def layout(cc):
            return (0, C, C + 1) if cc % CPE < CPE // 2 else (2, 0, 1)

        def weight_piece(j):
            if j < 8:
                w = W1C // 8
                return slice(j * w, (j + 1) * w), (j // 4, slice(j % 4 * w, (j % 4 + 1) * w))
            m = (j - 8) * (HM // 2)
            return slice(W1C + m * C, W1C + (m + HM // 2) * C), slice(m, m + HM // 2)

        def parts(j, e):
            cols, to = weight_piece(j)
            src = raw[e][:, cols]
            if j < 8:
                return src, w1_hi[e][:, to[0], to[1]], w1_lo[e][:, to[0], to[1]]
            return src.rearrange("p (m c) -> p m c", c=C), w2[e][:, to, 0, :], w2[e][:, to, 1, :]

        block = ctx.enter_context(nc.Block())

        @block.sync
        def _(sp):
            sp.dma_start(ident[:], d["ident"]).then_inc(s_id, 16)
            for e in range(2):
                sp.dma_start(raw[e][:], d["wexp"][e]).then_inc(s_raw[e], 16)
            chunk_rows = d["lists"].rearrange("(n p t) c -> n p t c", p=P, t=3)
            with sp.Fori(0, E // 2) as it:
                for cc in range(NC2):
                    if cc < 2:
                        sp.wait_ge(s_split, it * NC2 + cc if cc else it * NC2)
                    else:
                        sp.wait_ge(s_split, it * NC2 + (cc - 1))
                    sp.dma_start(rows[cc % 2][:], chunk_rows[it * NC2 + cc])\
                        .then_inc(s_rows[cc % 2], 16)
                    if cc % CPE == 2:
                        e = cc // CPE
                        sp.wait_ge(s_wlo, it * 20 + 10 * (e + 1))
                        sp.dma_start(raw[e][:], d["wexp"][it * 2 + (e + 2)]).then_inc(s_raw[e], 16)

        @block.gpsimd
        def _(pool):
            pool.memset(word_p[:], 0.0).then_inc(s_word, 1)
            pool.wait_ge(s_word, 1)
            words = Words(pool, word_p)
            pool.wait_ge(s_raw[0], 16)
            for j in range(10):
                src, hi, _ = parts(j, 0)
                pool.tensor_copy(hi, src).then_inc(s_whi, 1)

            def scatter(it, cc, t):
                n = 3 * cc + t
                words.wait((s_yout, it * (3 * NC2) + (n + 1)))
                q = 3 * (cc % 2) + t
                pool.indirect_dma_start(
                    d["y"][:, :], bass.IndirectOffsetOnAxis(ap=target[cc % 4][:, t:t + 1], axis=0),
                    yout[q][:], None, bounds_check=K2 * N - 1, oob_is_err=False)\
                    .then_inc(s_out[q], 16)

            def columns_twice(it, cc):
                q, (x0, _, _) = cc % 2, layout(cc)
                words.wait((s_rows[q], it * (NC2 // 2 * 16) + 16 * (cc // 2 + 1)),
                      (s_xt, it * NC2 + max(cc - 1, 0)))
                pool.tensor_copy(twice[q][:].rearrange("p t (a b) -> p t a b", a=2),
                                 rows[q][:, :, x0 + P:x0 + C].unsqueeze(2).broadcast_to([P, 3, 2, C2]))\
                    .then_inc(s_twice, 1)

            with pool.Fori(0, E // 2) as it:
                columns_twice(it, 0)
                for cc in range(NC2):
                    if cc + 1 < NC2:
                        columns_twice(it, cc + 1)
                    e, j = 1 - cc // CPE, cc % CPE
                    if j == 0:
                        pool.wait_ge(s_raw[e], (it + (1 if e else 2)) * 16)
                    words.wait((s_ug, it * (4 * NC2) + 4 * cc))
                    src, hi, _ = parts(j, e)
                    pool.tensor_copy(hi, src).then_inc(s_whi, 1)
                    if cc:
                        for t in range(3):
                            scatter(it, cc - 1, t)
                for t in range(3):
                    scatter(it, NC2 - 1, t)
            for q in range(6):
                pool.wait_ge(s_out[q], 16 * (E // 2) * (NC2 // 2))

        @block.tensor
        def _(pe):
            pe.wait_ge(s_id, 16)

            def turn_rows(it, cc):
                x0, _, _ = layout(cc)
                pe.wait_ge(s_rows[cc % 2], it * (NC2 // 2 * 16) + 16 * (cc // 2 + 1))
                for t in range(3):
                    pe.transpose(XT[0][:, t * P:(t + 1) * P], rows[cc % 2][:, t, x0:x0 + P], ident[:])
                pe.wait_ge(s_twice, it * NC2 + (cc + 1))
                for t in range(3):
                    mm = pe.transpose(XT[1][:, t * P:(t + 1) * P], twice[cc % 2][:, t, :], ident[:])
                mm.then_inc(s_xt, 1)

            def first(it, cc, m):
                n, q, e = 4 * cc + m, cc % 2, cc // CPE
                if m == 0:
                    pe.wait_ge(s_split, it * NC2 + (cc + 1))
                    if cc % CPE == 0:
                        pe.wait_ge(s_wlo, it * 20 + 10 * (e + 1))
                if n < 2:
                    pe.wait_ge(s_a, it * (4 * NC2))
                else:
                    pe.wait_ge(s_a, it * (4 * NC2) + (n - 1))
                for bank, c in ((GT[m % 2], HID + m * P), (UP[m % 2], m * P)):
                    w = slice(c, c + P)
                    for k, (a, b) in enumerate(((w1_hi[e][:, 0, w], x0_hi[q]), (w1_hi[e][:, 0, w], x0_lo[q]),
                                                (w1_lo[e][:, 0, w], x0_hi[q]), (w1_hi[e][:, 1, w], x1[q]),
                                                (w1_lo[e][:, 1, w], x1[q]))):
                        mm = pe.matmul(bank[:, 0:TILE3], a, b[:], start=(k == 0), stop=(k == 4))
                mm.then_inc(s_ug, 1)

            def second(it, cc, t):
                n, q, e = 3 * cc + t, cc % 2, cc // CPE
                if t == 0:
                    pe.wait_ge(s_alo, it * (4 * NC2) + 4 * (cc + 1))
                if n < 2:
                    pe.wait_ge(s_yout, it * (3 * NC2))
                else:
                    pe.wait_ge(s_yout, it * (3 * NC2) + (n - 1))
                c = slice(t * P, (t + 1) * P)
                y = Y[n % 2]
                for m in range(HM):
                    def wide():
                        return pe.matmul(y[:, 0:2 * C], a_hi[q][:, m, c],
                                         w2[e][:, m].rearrange("p a b -> p (a b)"),
                                         start=(m == 0), stop=(m == HM - 1))

                    if m < HM - 1:
                        wide()
                    pe.matmul(y[:, 0:C], a_lo[q][:, m, c], w2[e][:, m, 0], start=False, stop=False)
                    if m == HM - 1:
                        mm = wide()
                mm.then_inc(s_y, 1)

            with pe.Fori(0, E // 2) as it:
                turn_rows(it, 0)
                for cc in range(NC2):
                    for m in range(HM):
                        first(it, cc, m)
                        if cc and m < 3:
                            second(it, cc - 1, m)
                        if m == 1 and cc + 1 < NC2:
                            turn_rows(it, cc + 1)
                for t in range(3):
                    second(it, NC2 - 1, t)

        @block.scalar
        def _(act):
            def rows_hi(it, cc):
                act.wait_ge(s_xt, it * NC2 + (cc + 1))
                act.activation(x0_hi[cc % 2][:], XT[0][:, 0:TILE3], ACT.Copy).then_inc(s_xhi, 1)
                act.activation(x1[cc % 2][:], XT[1][:, 0:TILE3], ACT.Copy).then_inc(s_xhi, 1)

            def y_lo(it, cc, t):
                n = 3 * cc + t
                act.wait_ge(s_y, it * (3 * NC2) + (n + 1))
                act.activation(ylo[n % 2][:], Y[n % 2][:, C:2 * C], ACT.Copy,
                               scale=wt[cc % 4][:, t:t + 1]).then_inc(s_ylo, 1)

            def hidden_hi(it, cc, m):
                act.wait_ge(s_a, it * (4 * NC2) + (4 * cc + m + 1))
                act.activation(a_hi[cc % 2][:, m], a32[m % 2][:], ACT.Copy).then_inc(s_ahi, 1)

            with act.Fori(0, E // 2) as it:
                rows_hi(it, 0)
                for cc in range(NC2):
                    for m in range(HM):
                        act.wait_ge(s_ug, it * (4 * NC2) + (4 * cc + m + 1))
                        act.activation(gate[m % 2][:], GT[m % 2][:, 0:TILE3], ACT.Silu).then_inc(s_gate, 1)
                        if cc and m < 3:
                            y_lo(it, cc - 1, m)
                        if m:
                            hidden_hi(it, cc, m - 1)
                        if m == 1 and cc + 1 < NC2:
                            rows_hi(it, cc + 1)
                    hidden_hi(it, cc, HM - 1)
                for t in range(3):
                    y_lo(it, NC2 - 1, t)

        @block.vector
        def _(dve):
            def split_piece(k, j, e):
                dve.wait_ge(s_whi, k)
                src, hi, lo = parts(j, e)
                dve.tensor_tensor(lo, src, hi.bitcast(F32), ALU.subtract).then_inc(s_wlo, 1)

            for j in range(10):
                split_piece(j + 1, j, 0)

            def rows_lo(it, cc):
                q, (x0, w, to) = cc % 2, layout(cc)
                dve.wait_ge(s_rows[q], it * (NC2 // 2 * 16) + 16 * (cc // 2 + 1))
                if cc >= 4:
                    for t in range(3):
                        dve.wait_ge(s_out[3 * q + t], it * (NC2 // 2 * 16) + 16 * (cc // 2 - 1))
                else:
                    for t in range(3):
                        dve.wait_ge(s_out[3 * q + t], it * (NC2 // 2 * 16))
                dve.tensor_copy(wt[cc % 4][:], rows[q][:, :, w])
                dve.tensor_copy(target[cc % 4][:], rows[q][:, :, to])
                dve.wait_ge(s_xhi, it * (2 * NC2) + (2 * cc + 2))
                dve.tensor_tensor(x0_lo[q][:], XT[0][:, 0:TILE3], x0_hi[q][:].bitcast(F32), ALU.subtract)
                dve.tensor_tensor(x1[q][C2:P, :], XT[1][C2:P, 0:TILE3], x1[q][C2:P, :].bitcast(F32),
                                  ALU.subtract).then_inc(s_split, 1)

            def y_out(it, cc, t):
                n, q = 3 * cc + t, 3 * (cc % 2) + t
                dve.wait_ge(s_ylo, it * (3 * NC2) + (n + 1))
                dve.wait_ge(s_out[q], it * (NC2 // 2 * 16) + 16 * (cc // 2)) if cc >= 2 else \
                    dve.wait_ge(s_out[q], it * (NC2 // 2 * 16))
                dve.scalar_tensor_tensor(out=yout[q][:], in0=Y[n % 2][:, 0:C], scalar=wt[cc % 4][:, t:t + 1],
                                         in1=ylo[n % 2][:], op0=ALU.mult, op1=ALU.add).then_inc(s_yout, 1)

            def hidden_lo(it, cc, m):
                dve.wait_ge(s_ahi, it * (4 * NC2) + (4 * cc + m + 1))
                dve.tensor_tensor(a_lo[cc % 2][:, m], a32[m % 2][:], a_hi[cc % 2][:, m].bitcast(F32),
                                  ALU.subtract).then_inc(s_alo, 1)

            with dve.Fori(0, E // 2) as it:
                rows_lo(it, 0)
                for cc in range(NC2):
                    for m in range(HM):
                        dve.wait_ge(s_alo, it * (4 * NC2) + max(4 * cc + m - 1, 0))
                        dve.wait_ge(s_gate, it * (4 * NC2) + (4 * cc + m + 1))
                        dve.tensor_tensor(a32[m % 2][:], UP[m % 2][:, 0:TILE3], gate[m % 2][:], ALU.mult)\
                            .then_inc(s_a, 1)
                        if cc and m < 3:
                            y_out(it, cc - 1, m)
                        if m:
                            hidden_lo(it, cc, m - 1)
                        if m == 1 and cc + 1 < NC2:
                            rows_lo(it, cc + 1)
                    split_piece(it * 20 + (10 + cc + 1), cc % CPE, 1 - cc // CPE)
                    hidden_lo(it, cc, HM - 1)
                for t in range(3):
                    y_out(it, NC2 - 1, t)


def last_block(nc, d, out):
    TPP = 6
    NB = 4
    NCH = N // (P * TPP) // NB * NB
    REST = N - NCH * P * TPP
    RT = 5
    RP = REST // RT
    assert RP * RT == REST and RP <= P
    with ExitStack() as ctx:
        def sb(name, shape, dt):
            return ctx.enter_context(nc.sbuf_tensor(name, shape, dt))

        def sem(name):
            return ctx.enter_context(nc.semaphore(name))

        a, y0, y1, o = ([sb(f"t_{name}_{n}", [P, TPP, C], F32) for n in range(NB)]
                        for name in ("x", "y0", "y1", "o"))
        stats = [sb(f"t_stats{n}", [P, TPP, 6], F32) for n in range(NB)]
        mv = [sb(f"t_mv{n}", [P, TPP, 2], F32) for n in range(NB)]
        var, rstd, shift = ([sb(f"t_{name}_{n}", [P, TPP], F32) for n in range(NB)]
                            for name in ("var", "rstd", "shift"))
        half = sb("t_half", [P, TPP], F32)
        word_v = sb("t_word", [1, NWORDS], F32)
        s_in = [sem(f"t_loaded{n}") for n in range(NB)]
        s_half, s_sum, s_all = sem("t_half_ready"), sem("first_sum"), sem("sum_ready")
        s_stat, s_mv, s_var, s_rstd = sem("t_stats"), sem("t_mean"), sem("t_variance"), sem("t_rstd")
        s_shift, s_o = sem("t_shift"), sem("t_out_ready")
        s_st = [sem(f"t_stored{n}") for n in range(NB)]
        block = ctx.enter_context(nc.Block())

        def views(ap, first):
            return ap[first:first + NCH * P * TPP, :].rearrange("(n p t) c -> n p t c", p=P, t=TPP)

        def rest(ap, first):
            return ap[first + N - REST:first + N, :].rearrange("(p t) c -> p t c", t=RT)

        x_v, y0_v, y1_v, out_v = (views(ap, f) for ap, f in
                                  ((d["x1"], 0), (d["y"], 0), (d["y"], N), (out, 0)))

        def chunks(eng, body):
            for c in range(NB):
                body(c, 0, c, P, TPP)
            with eng.Fori(1, NCH // NB) as it:
                for q in range(NB):
                    body(it * NB + q, it, q, P, TPP)
            body(NCH, NCH // NB, 0, RP, RT)

        @block.sync
        def _(sp):
            def body(c, turn, q, rows, t):
                wait(sp, s_o, c - (NB - 1))
                for dst, v, ap, f in ((a, x_v, d["x1"], 0), (y0, y0_v, d["y"], 0), (y1, y1_v, d["y"], N)):
                    src = v[c] if rows == P else rest(ap, f)
                    sp.dma_start(dst[q][0:rows, 0:t, :], src).then_inc(s_in[q], 16)
            chunks(sp, body)

        @block.gpsimd
        def _(pool):
            pool.memset(half[:], -0.5).then_inc(s_half, 1)
            pool.memset(word_v[:], 0.0).then_inc(s_half, 1)
            pool.wait_ge(s_half, 2)

            def power(c, q, rows, t):
                pool.wait_ge(s_var, c + 1)
                wait(pool, s_o, c - (NB - 1))
                pool.tensor_tensor(rstd[q][0:rows, 0:t], var[q][0:rows, 0:t], half[0:rows, 0:t],
                                   ALU.pow).then_inc(s_rstd, 1)

            def body(c, turn, q, rows, t):
                pool.wait_ge(s_in[q], (turn + 1) * 48)
                pool.tensor_tensor(a[q][0:rows, 0:t], a[q][0:rows, 0:t], y0[q][0:rows, 0:t],
                                   ALU.add).then_inc(s_sum, 1)
                if not isinstance(c, int) or c:
                    power(c - 1, (q - 1) % NB, P, TPP)
            chunks(pool, body)
            power(NCH, 0, RP, RT)

        @block.vector
        def _(dve):
            words = Words(dve, word_v)
            dve.wait_ge(s_half, 2)

            def turned_mean(c, q, rows, t):
                dve.wait_ge(s_rstd, c + 1)
                dve.scalar_tensor_tensor(out=shift[q][0:rows, 0:t], in0=mv[q][0:rows, 0:t, 0], scalar=-1.0,
                                         in1=rstd[q][0:rows, 0:t], op0=ALU.mult, op1=ALU.mult)\
                    .then_inc(s_shift, 1)

            def body(c, turn, q, rows, t):
                dve.wait_ge(s_sum, c + 1)
                dve.tensor_tensor(a[q][0:rows, 0:t], a[q][0:rows, 0:t], y1[q][0:rows, 0:t],
                                  ALU.add).then_inc(s_all, 1)
                dve.wait_ge(s_all, c + 1)
                for n in range(t):
                    ins = dve.bn_stats(stats[q][0:rows, n, :], a[q][0:rows, n, :])
                ins.then_inc(s_stat, 1)
                if not isinstance(c, int) or c:
                    turned_mean(c - 1, (q - 1) % NB, P, TPP)
                words.wait((s_stat, c + 1), (s_o, c - (NB - 1)))
                for n in range(t):
                    ins = dve.bn_aggr(mv[q][0:rows, n, :], stats[q][0:rows, n, :])
                ins.then_inc(s_mv, 1)
                dve.wait_ge(s_mv, c + 1)
                dve.tensor_scalar(var[q][0:rows, 0:t], mv[q][0:rows, 0:t, 1], EPS, None, ALU.add)\
                    .then_inc(s_var, 1)
            chunks(dve, body)
            turned_mean(NCH, 0, RP, RT)

        @block.scalar
        def _(act):
            def body(c, turn, q, rows, t):
                wait(act, s_st[q], turn * 16)
                act.wait_ge(s_shift, c + 1)
                for n in range(t):
                    ins = act.activation(o[q][0:rows, n, :], a[q][0:rows, n, :], ACT.Identity,
                                         bias=shift[q][0:rows, n:n + 1], scale=rstd[q][0:rows, n:n + 1])
                ins.then_inc(s_o, 1)
                act.wait_ge(s_o, c + 1)
                dst = out_v[c] if rows == P else rest(out, 0)
                act.dma_start(dst, o[q][0:rows, 0:t, :]).then_inc(s_st[q], 16)
            chunks(act, body)
            for q in range(NB):
                act.wait_ge(s_st[q], (NCH // NB + (q == 0)) * 16)


def build(nc, d, out):
    d = dict(d)
    d["x1"] = nc.dram_tensor("x1_tokens", [N, C], F32).ap()
    d["lists"] = nc.dram_tensor("expert_lists", [NSLOT, ROW], F32).ap()
    d["y"] = nc.dram_tensor("expert_results", [K2 * N, C], F32).ap()
    attention_block(nc, d)
    expert_block(nc, d)
    last_block(nc, d, out)


def kernel(x, L0_tok_W, L0_tok_b, L0_tok_class_token, L0_tok_pos_emb, L0_attn_w_attn,
           L0_attn_b_attn, L0_attn_w_proj, L0_attn_b_proj, L0_ffn_Wg, L0_ffn_W1, L0_ffn_W2):
    import ml_dtypes
    import numpy as np
    import concourse.bacc as bacc
    from concourse.bass_utils import run_bass_kernel_spmd

    f32, bf16 = np.float32, ml_dtypes.bfloat16
    ins = {}

    px = np.asarray(x).reshape(B, 14, 16, 14, 16, 3).transpose(2, 4, 5, 0, 1, 3)
    px = px.reshape(KT, P, NPAIR, 2, T - 1)
    xt = np.zeros((NPAIR + 2, P, KT, 2, TI), f32)
    xt[:NPAIR, ..., 1:T] = px.transpose(2, 1, 0, 3, 4)
    ins["xt"] = xt.reshape(NPAIR + 2, P, KT, TP)
    twice = np.concatenate([np.arange(C), np.arange(P, C)])
    ins["wtok"] = np.asarray(L0_tok_W)[:, twice].reshape(KT, P, 2 * P).transpose(1, 0, 2)

    def feature_tiles(w):
        return np.stack([w[:P], np.concatenate([w[P:], w[P:]])], axis=1)

    heads = np.arange(C).reshape(3, 64)
    order = np.concatenate([np.concatenate([g, C + g]) for g in heads] + [2 * C + np.arange(C)])
    wa, ba = np.asarray(L0_attn_w_attn)[:, order], np.asarray(L0_attn_b_attn)[order]
    wp, bp = np.asarray(L0_attn_w_proj), np.asarray(L0_attn_b_proj)
    wa = np.concatenate([wa, np.eye(C, dtype=f32)], axis=1)
    ins["raw"] = np.concatenate([feature_tiles(wa).reshape(P, -1), feature_tiles(wp).reshape(P, -1)], axis=1)
    ins["bqk"] = ba[:2 * C].reshape(3, P).T
    ins["bvp"] = np.broadcast_to(np.concatenate([ba[2 * C:], bp]), (P, 2 * C))

    def image_columns(t):
        full = np.zeros((C, TI), f32)
        full[:, :T] = t.T
        return feature_tiles(full)

    ins["pos"] = image_columns(np.asarray(L0_tok_pos_emb))
    ins["bias"] = image_columns(np.concatenate([np.asarray(L0_tok_class_token)[None],
                                                np.broadcast_to(np.asarray(L0_tok_b), (T - 1, C))]))
    wg = np.asarray(L0_ffn_Wg)
    ins["wg0"], ins["wg1"] = wg[:P], wg[P:]

    w1, w2 = np.asarray(L0_ffn_W1), np.asarray(L0_ffn_W2)
    wexp = np.stack([np.concatenate([
        feature_tiles(w1[e % E]).reshape(P, -1),
        w2[e % E].reshape(HM, P, C).transpose(1, 0, 2).reshape(P, -1)], axis=1) for e in range(E + 2)])
    ins["wexp"] = wexp

    sel = np.zeros((P, 2, 2, 2, P), bf16)
    for jj in range(2):
        for hh in range(2):
            for r in range(4):
                for e in range(HD):
                    src, dst = HD * (2 * jj + hh) + e, 64 * hh + HD * r + e
                    sel[src, 0, jj, r % 2, dst] = 1
                    sel[64 + src, 1, jj, r // 2, dst] = 1
    ins["sel"] = sel.reshape(P, 8 * P)
    n = np.arange(P)
    ins["ident"] = np.eye(P, dtype=f32)
    ins["masks"] = np.stack([np.eye(P), np.where(n[None] > n[:, None], -1e30, 0.0), np.ones((P, P)),
                             n[:, None] < n[None]], axis=1).astype(bf16)
    ins["iota8"] = np.broadcast_to(np.arange(E, dtype=f32), (P, E))
    ins["kbase"] = np.broadcast_to(np.arange(K2, dtype=f32) * SEG, (P, 4, K2))
    ins["valid"] = np.stack([n < r for r in REAL], axis=1).astype(f32)
    ins["tid"] = np.stack([im * T + hf * P + n for im, hf, _, _ in TILES], axis=1).astype(f32)

    nc = bacc.Bacc("TRN2", target_bir_lowering=False, num_devices=1)
    arrays, d = {}, {}
    for name, value in ins.items():
        arrays[f"in_{name}"] = np.ascontiguousarray(value)
        d[name] = nc.dram_tensor(f"in_{name}", value.shape, mybir.dt.from_np(value.dtype),
                                 kind="ExternalInput").ap()
    out = nc.dram_tensor("out", [N, C], F32, kind="ExternalOutput").ap()
    build(nc, d, out)
    r = run_bass_kernel_spmd(nc, [arrays], core_ids=[0])
    return r.results[0]["out"].reshape(B, T, C)
```
